# Optimizing a Trainium2 kernel written in Bass

```python
import numpy as np
import jax
import jax.numpy as jnp

def _softmax(x, axis=-1):
    return jax.nn.softmax(x, axis=axis)

def _gelu(x):
    return jax.nn.gelu(x, approximate=True)

def _silu(x):
    return jax.nn.silu(x)

def _sigmoid(x):
    return jax.nn.sigmoid(x)

def _layernorm(x, axis=-1, eps=1e-05):
    m = jnp.mean(x, axis=axis, keepdims=True)
    v = jnp.var(x, axis=axis, keepdims=True)
    return (x - m) / jnp.sqrt(v + eps)

def _scatter_add(tgt, idx, src, axis=0):
    return tgt.at[idx].add(src)

def _segment_sum(src, seg, n):
    return jax.ops.segment_sum(src, seg, n)
kernel_name = 'mk_xattn_seq_d1_seqx_r4_ac4c1b'

def setup_inputs(seed: int=0):
    np.random.seed(seed)
    _w = jnp.asarray

    def _rec_inputs():
        import jax
        import jax.numpy as jnp
        _rk = jax.random.key(seed)
        x = -0.0002928 + 1 * jax.random.normal(jax.random.fold_in(_rk, 1), (8, 256, 256), jnp.float32)
        _lenS = 256 - jax.random.randint(jax.random.fold_in(_rk, 7), (8,), 0, max(1, 256 // 4) + 1, jnp.int32)
        _lenS2 = 256 - jax.random.randint(jax.random.fold_in(_rk, 8), (8,), 0, max(1, 256 // 4) + 1, jnp.int32)
        _ctx_768P = jax.random.normal(jax.random.fold_in(_rk, 11), (8, 16, 192), jnp.float32)
        _ctx_768c = jax.random.dirichlet(jax.random.fold_in(_rk, 511), 0.3 * jnp.ones((16,), jnp.float32), (8, 256))
        _ctx_768t = jnp.einsum('bsk,bkd->bsd', _ctx_768c, _ctx_768P)
        _ctx_768t = _ctx_768t * jax.lax.rsqrt(jnp.mean(jnp.square(_ctx_768t)) + 1e-12) * 0.953939
        ctx_768 = 2.09791e-05 + 1.00001 * (_ctx_768t + 0.3 * jax.random.normal(jax.random.fold_in(_rk, 611), (8, 256, 192), jnp.float32))
        return (x, ctx_768)
    x, ctx_768 = _rec_inputs()

    def _L0_xattn_setup():
        import jax, jax.numpy as jnp
        import numpy as np
        D_Q, D_CTX, N_HEADS, HEAD_DIM = (256, 192, 16, 64)
        INNER = N_HEADS * HEAD_DIM
        EPS = 1e-05

        def _layernorm(x, gamma, beta):
            mu = jnp.mean(x, axis=-1, keepdims=True)
            var = jnp.var(x, axis=-1, keepdims=True)
            return (x - mu) * jax.lax.rsqrt(var + EPS) * gamma + beta
        key = jax.random.key(seed)
        ks = jax.random.split(key, 8)
        B, NQ, NC = (4, 256, 256)
        s_q = 1.0 / np.sqrt(D_Q)
        s_c = 1.0 / np.sqrt(D_CTX)
        s_i = 1.0 / np.sqrt(INNER)
        return {'x': jax.random.normal(ks[0], (B, NQ, D_Q), jnp.float32), 'context': jax.random.normal(ks[1], (B, NC, D_CTX), jnp.float32), 'Wq': jax.random.normal(ks[2], (D_Q, INNER), jnp.float32) * s_q, 'Wk': jax.random.normal(ks[3], (D_CTX, INNER), jnp.float32) * s_c, 'Wv': jax.random.normal(ks[4], (D_CTX, INNER), jnp.float32) * s_c, 'Wo': jax.random.normal(ks[5], (INNER, D_Q), jnp.float32) * s_i, 'bo': jnp.zeros((D_Q,), jnp.float32), 'gamma': jnp.ones((D_Q,), jnp.float32), 'beta': jnp.zeros((D_Q,), jnp.float32)}
    _L0_xattn_all = _L0_xattn_setup()
    _L0_xattn_in = {k: v for k, v in _L0_xattn_all.items() if k in ('Wq', 'Wk', 'Wv', 'Wo', 'bo', 'gamma', 'beta')}
    del _L0_xattn_all
    return {'x': x, 'ctx_768': ctx_768, 'L0_xattn_Wq': _L0_xattn_in['Wq'], 'L0_xattn_Wk': _L0_xattn_in['Wk'], 'L0_xattn_Wv': _L0_xattn_in['Wv'], 'L0_xattn_Wo': _L0_xattn_in['Wo'], 'L0_xattn_bo': _L0_xattn_in['bo'], 'L0_xattn_gamma': _L0_xattn_in['gamma'], 'L0_xattn_beta': _L0_xattn_in['beta']}

def reference(x, ctx_768, L0_xattn_Wq, L0_xattn_Wk, L0_xattn_Wv, L0_xattn_Wo, L0_xattn_bo, L0_xattn_gamma, L0_xattn_beta):
    import jax
    import jax.numpy as jnp

    def _L0_xattn_ref(x, context, Wq, Wk, Wv, Wo, bo, gamma, beta):
        import jax, jax.numpy as jnp
        import numpy as np
        D_Q, D_CTX, N_HEADS, HEAD_DIM = (256, 192, 16, 64)
        INNER = N_HEADS * HEAD_DIM
        EPS = 1e-05

        def _layernorm(x, gamma, beta):
            mu = jnp.mean(x, axis=-1, keepdims=True)
            var = jnp.var(x, axis=-1, keepdims=True)
            return (x - mu) * jax.lax.rsqrt(var + EPS) * gamma + beta
        scale = HEAD_DIM ** (-0.5)
        h = _layernorm(x, gamma, beta)
        B, NQ, _ = x.shape
        NC = context.shape[1]
        Q = (h @ Wq).reshape(B, NQ, N_HEADS, HEAD_DIM)
        K = (context @ Wk).reshape(B, NC, N_HEADS, HEAD_DIM)
        V = (context @ Wv).reshape(B, NC, N_HEADS, HEAD_DIM)
        attn = jnp.einsum('bihd,bjhd->bhij', Q, K)
        attn = jax.nn.softmax(attn, axis=-1) * scale
        vals = jnp.einsum('bhij,bjhd->bihd', attn, V).reshape(B, NQ, INNER)
        out = vals @ Wo + bo
        return x + out
    x = _L0_xattn_ref(x, ctx_768, L0_xattn_Wq, L0_xattn_Wk, L0_xattn_Wv, L0_xattn_Wo, L0_xattn_bo, L0_xattn_gamma, L0_xattn_beta)
    return x

_drawn_inputs = setup_inputs


def setup_inputs(seed=0):
    import zlib

    import numpy as np

    out = dict(_drawn_inputs(seed))
    spreads = {'L0_xattn_bo': (0.0, 0.1), 'L0_xattn_gamma': (1.0, 0.2), 'L0_xattn_beta': (0.0, 0.309)}
    factors = {}
    for name, (base, spread) in spreads.items():
        noise = np.random.default_rng([zlib.crc32(name.encode()), seed]).standard_normal(out[name].shape)
        drawn = base * np.exp(spread * noise) if base else spread * noise
        out[name] = jnp.asarray(drawn.astype(out[name].dtype))
    for name, factor in factors.items():
        out[name] = (out[name] * factor).astype(out[name].dtype)
    return out
```

```python
import concourse.bass as bass
from concourse import mybir
from contextlib import ExitStack


def cross_attention_block(nc, x, ctx_in, w_q, w_k, w_v, w_o, b_o, gamma, beta, out):
    fp32 = mybir.dt.float32
    fp32r = mybir.dt.float32r
    ALU = mybir.AluOpType
    ACT = mybir.ActivationFunctionType
    AX = mybir.AxisListType.X

    P = 128
    SEQS, ROWS, D = x.shape
    D_CTX = ctx_in.shape[2]
    INNER = w_q.shape[1]
    HEAD = 64
    HALF = P // 2
    PAIRS = INNER // P
    STEPS = SEQS * PAIRS
    RT = ROWS // P
    DT = D // P
    EPS = 1e-5
    SCALE = HEAD ** -0.5
    GROUP = 4
    RING = 4
    PROJECT, MIX, OUT = 2, 2, 3
    LOOP_FROM, LOOP_STEPS, LOOPS = 4, 2 * PAIRS, 3
    FIRST, LAST = -11, STEPS + OUT

    CT = 2 * D_CTX // P
    CREST = D_CTX - P

    x_v = x.rearrange("b (r p) d -> b p r d", p=P)
    c_v = ctx_in.rearrange("b (r p) d -> b p r d", p=P)
    y_v = out.rearrange("b (r p) d -> b p r d", p=P)

    Q0, K0, V0, O0, CHUNKS = 0, 2, 5, 8, 10
    LO_OF = {0: 0, 1: 1, 2: 2, 3: 3, 5: 4, 6: 5, 8: 6, 9: 7}
    RAWS = 5

    with ExitStack() as ctx:
        def sb(name, shape, dt=fp32):
            return ctx.enter_context(nc.sbuf_tensor(name, shape, dt))

        def bank(name):
            return ctx.enter_context(nc.psum_tensor(name, [P, 512], fp32))

        def sem(name):
            return ctx.enter_context(nc.semaphore(name))

        w_raw = sb("w_raw", [P, RAWS, INNER])
        w_hi = sb("w_hi", [P, CHUNKS, INNER], fp32r)
        w_lo = sb("w_lo", [P, len(LO_OF), INNER], fp32r)
        ident = sb("ident", [P, P])
        gamma_c = sb("gamma_c", [P, DT])
        beta_c = sb("beta_c", [P, DT])
        bo_b = sb("bo_b", [P, D])
        neg_half = sb("neg_half", [P, RT])
        x_in = sb("x_in", [P, 2, RT, D])
        c_in = sb("c_in", [P, 2, RT, D_CTX])
        bn = sb("bn", [P, RT, 6])
        mean_var = sb("mean_var", [P, RT, 2])
        var_eps = sb("var_eps", [P, RT])
        rstd = sb("rstd", [P, RT])
        x_norm = sb("x_norm", [P, RT, D])
        x_bias = sb("x_bias", [P, 2, RT, D])
        c_split = sb("c_split", [P, RT, 2 * D_CTX], fp32r)
        h_full = sb("h_full", [P, DT, ROWS])
        h_hi = sb("h_hi", [P, 2, DT, ROWS], fp32r)
        h_lo = sb("h_lo", [P, 2, DT, ROWS], fp32r)
        c_t = sb("c_t", [P, 2, CT, ROWS], fp32r)
        stack = sb("stack", [P, RING * 2, 3, ROWS], fp32r)
        v_sb = sb("v_sb", [P, 2, RT, GROUP * P])
        neg_max = sb("neg_max", [P, RING * 2, RT])
        sums = sb("sums", [P, RING * 2, RT])
        inv = sb("inv", [P, RING * 2, RT])
        prob = sb("prob", [P, RING * 2, RT, ROWS])
        prob_t = sb("prob_t", [P, 2, 2, RT, ROWS])
        mix_hi = sb("mix_hi", [P, 2, ROWS], fp32r)
        mix_lo = sb("mix_lo", [P, 2, ROWS], fp32r)
        y_sb = sb("y_sb", [P, 2, RT, D])

        qk_ps = bank("qk_ps")
        misc_ps = bank("misc_ps")
        s_ps = [bank("s_even_ps"), bank("s_odd_ps")]
        pt_ps = [bank("pt_even_ps"), bank("pt_odd_ps")]
        mix_ps = bank("mix_ps")
        o_ps = bank("o_ps")

        w_in = [sem(f"w_in{i}") for i in range(CHUNKS)]
        x_loaded = [sem("x_loaded0"), sem("x_loaded1")]
        c_loaded = [sem("c_loaded0"), sem("c_loaded1")]
        small_in = sem("small_in")
        ident_zero = sem("ident_zero")
        consts_ready = sem("consts_ready")
        w_hi_ready = sem("w_hi_ready")
        w_lo_ready = sem("w_lo_ready")
        stats_done = sem("stats_done")
        aggr_done = sem("aggr_done")
        var_ready = sem("var_ready")
        rstd_ready = sem("rstd_ready")
        x_norm_ready = sem("x_norm_ready")
        x_bias_ready = sem("x_bias_ready")
        c_hi_ready = sem("c_hi_ready")
        c_split_ready = sem("c_split_ready")
        x_turned = sem("x_turned")
        c_turned = sem("c_turned")
        h_full_ready = sem("h_full_ready")
        h_hi_ready = sem("h_hi_ready")
        h_lo_ready = sem("h_lo_ready")
        c_t_ready = sem("c_t_ready")
        projected = sem("projected")
        hi_ready = sem("hi_ready")
        lo_ready = sem("lo_ready")
        twice = [sem(f"twice{i}") for i in range(RING)]
        v_made = sem("v_made")
        v_ready = [sem("v_ready0"), sem("v_ready1")]
        scores_made = sem("scores_made")
        max_ready = sem("max_ready")
        prob_ready = sem("prob_ready")
        inv_ready = sem("inv_ready")
        scaled = sem("scaled")
        turned = sem("turned")
        prob_t_ready = [sem("prob_t_ready_even"), sem("prob_t_ready_odd")]
        mixed = sem("mixed")
        mix_hi_ready = sem("mix_hi_ready")
        mix_lo_ready = sem("mix_lo_ready")
        o_added = sem("o_added")
        y_ready = sem("y_ready")
        y_free = [sem("y_free0"), sem("y_free1")]

        block = ctx.enter_context(nc.Block())

        def when(s, offset, every, count):
            n, rest = divmod(s - offset, every)
            return n if rest == 0 and 0 <= n < count else None

        def slot(n, ring):
            return n % ring

        def walk(engine, step):
            for s in range(FIRST, LOOP_FROM):
                step(s, lambda n: 0)
            with engine.Fori(0, LOOPS) as turn:
                for s in range(LOOP_FROM, LOOP_FROM + LOOP_STEPS):
                    step(s, lambda n: turn * n)
            for s in range(LOOP_FROM + LOOP_STEPS * LOOPS, LAST):
                step(s, lambda n: 0)

        LOAD, STATS, SPLIT_C, TURN_X, TURN_C, BIAS_X, TURN_C2 = -12, -11, -9, -8, -7, -5, -4
        PUT = PAIRS - 1 + OUT

        @block.sync
        def _(sp):
            def load_weight(i):
                if i >= RAWS:
                    sp.wait_ge(w_hi_ready, i - RAWS + 1)
                    sp.wait_ge(w_lo_ready, sum(1 for c in LO_OF if c <= i - RAWS))
                dst = w_raw[:, i % RAWS, :]
                if i < K0:
                    sp.dma_start(dst, w_q[i * P:(i + 1) * P, :]).then_inc(w_in[i], 16)
                elif i < O0:
                    w, k = (w_k, i - K0) if i < V0 else (w_v, i - V0)
                    if k == 0:
                        sp.dma_start(dst, w[0:P, :]).then_inc(w_in[i], 16)
                    elif k == 1:
                        sp.dma_start(dst[0:CREST, :], w[P:D_CTX, :]).then_inc(w_in[i], 16)
                        sp.dma_start(dst[CREST:P, :], w[0:P - CREST, :]).then_inc(w_in[i], 16)
                    else:
                        sp.dma_start(dst, w[D_CTX - P:D_CTX, :]).then_inc(w_in[i], 16)
                else:
                    rows = w_o[(i - O0) * GROUP * P:(i - O0 + 1) * GROUP * P, :]
                    sp.dma_start(dst.rearrange("p (g n) -> p g n", g=GROUP),
                                 rows.rearrange("(g p) n -> p g n", p=P)).then_inc(w_in[i], 16)

            def load_rows(b, sequence):
                k = slot(b, 2)
                sp.dma_start(x_in[:, k, :, :], x_v[sequence]).then_inc(x_loaded[k], 16)
                sp.dma_start(c_in[:, k, :, :], c_v[sequence]).then_inc(c_loaded[k], 16)

            def number(n):
                return n if isinstance(n, int) else sp.snap(n)

            load_rows(0, 0)
            load_weight(0)
            load_weight(1)
            sp.dma_start(gamma_c[:, :], gamma.rearrange("(t p) -> p t", p=P),
                         allow_slow_non_contiguous=True).then_inc(small_in, 16)
            sp.dma_start(beta_c[:, :], beta.rearrange("(t p) -> p t", p=P),
                         allow_slow_non_contiguous=True).then_inc(small_in, 16)
            sp.dma_start(bo_b[:, :], b_o.partition_broadcast(P)).then_inc(small_in, 16)
            for i in range(K0, V0):
                load_weight(i)
            load_rows(1, 1)
            for i in range(V0, CHUNKS):
                load_weight(i)

            def step(s, turns):
                b = when(s, LOAD, PAIRS, SEQS)
                if b is not None and b >= 2:
                    sequence, used = number(b + turns(2)), number(b - 1 + turns(2))
                    sp.wait_ge(x_norm_ready, used)
                    sp.wait_ge(x_bias_ready, used)
                    sp.wait_ge(c_split_ready, used)
                    load_rows(b, sequence)
                t = when(s, -PROJECT, 1, STEPS)
                if t is not None:
                    for h in range(2):
                        k = slot(t, RING) * 2 + h
                        own = slice(h * HALF, (h + 1) * HALF)
                        other = slice((1 - h) * HALF, (2 - h) * HALF)
                        split = number(4 * t + 1 + h + turns(64))
                        sp.wait_ge(lo_ready, split)
                        sp.dma_start(stack[other, k, 1:3, :].bitcast(fp32),
                                     stack[own, k, 1:3, :].bitcast(fp32))\
                            .then_inc(twice[slot(t, RING)], 16)
                b = when(s, PUT, PAIRS, SEQS)
                if b is not None:
                    sequence, added = number(b + turns(2)), number(b + 1 + turns(2))
                    sp.wait_ge(y_ready, added)
                    sp.dma_start(y_v[sequence], y_sb[:, slot(b, 2), :, :])\
                        .then_inc(y_free[slot(b, 2)], 16)

            walk(sp, step)
            for k in range(2):
                sp.wait_ge(y_free[k], 16 * (SEQS // 2 + 1))

        @block.gpsimd
        def _(pool):
            nc.gpsimd.memset(ident[:, :], 0.0).then_inc(ident_zero, 1)
            nc.gpsimd.memset(neg_half[:, :], -0.5).then_inc(ident_zero, 1)
            pool.wait_ge(ident_zero, 2)
            nc.gpsimd.affine_select(out=ident[:, :], in_=ident[:, :], compare_op=ALU.not_equal,
                                    fill=1.0, base=0, pattern=[[-1, P]], channel_multiplier=1)\
                .then_inc(consts_ready, 1)

            def step(s, turns):
                t = when(s, 0, 1, STEPS)
                if t is not None:
                    for h in range(2):
                        k = slot(t, RING) * 2 + h
                        pool.wait_ge(inv_ready, 2 * t + h + 1 + turns(32))
                        for r in range(RT):
                            last = nc.gpsimd.tensor_scalar(prob[:, k, r, :], prob[:, k, r, :],
                                                           inv[:, k, r:r + 1], SCALE,
                                                           ALU.mult, ALU.mult)
                        last.then_inc(scaled, 1)
                b = when(s, STATS, PAIRS, SEQS)
                if b is not None:
                    pool.wait_ge(var_ready, b + 1 + turns(2))
                    if b >= 1:
                        pool.wait_ge(x_turned, b + turns(2))
                    nc.gpsimd.tensor_tensor(rstd[:, :], var_eps[:, :], neg_half[:, :], ALU.pow)\
                        .then_inc(rstd_ready, 1)
                    pool.wait_ge(rstd_ready, b + 1 + turns(2))
                    for r in range(RT):
                        last = nc.gpsimd.tensor_scalar(x_norm[:, r, :], x_in[:, slot(b, 2), r, :],
                                                       mean_var[:, r, 0:1], rstd[:, r:r + 1],
                                                       ALU.subtract, ALU.mult)
                    last.then_inc(x_norm_ready, 1)
                b = when(s, BIAS_X, PAIRS, SEQS)
                if b is not None:
                    if b == 0:
                        pool.wait_ge(small_in, 48)
                    if b >= 2:
                        pool.wait_ge(y_ready, b - 1 + turns(2))
                    for r in range(RT):
                        last = nc.gpsimd.tensor_tensor(x_bias[:, slot(b, 2), r, :],
                                                       x_in[:, slot(b, 2), r, :], bo_b[:, :],
                                                       ALU.add)
                    last.then_inc(x_bias_ready, 1)

            for s in range(FIRST, LAST):
                step(s, lambda n: 0)

        @block.scalar
        def _(act):
            def weight_hi(i):
                act.wait_ge(w_in[i], 32 if i in (K0 + 1, V0 + 1) else 16)
                nc.scalar.activation(w_hi[:, i, :], w_raw[:, i % RAWS, :], ACT.Copy)\
                    .then_inc(w_hi_ready, 1)

            def step(s, turns):
                if s == TURN_X - 2:
                    for i in range(Q0, K0):
                        weight_hi(i)
                if s == TURN_C2 - 1:
                    for i in range(K0, V0):
                        weight_hi(i)
                if s == TURN_C2 + 1:
                    for i in range(V0, CHUNKS):
                        weight_hi(i)

                for h in range(2):
                    t = when(s, 0, 1, STEPS)
                    if t is not None:
                        k = slot(t, RING) * 2 + h
                        if t >= RING:
                            act.wait_ge(turned, 2 * (t - RING) + h + 1 + turns(32))
                        act.wait_ge(max_ready, 2 * t + h + 1 + turns(32))
                        for r in range(RT):
                            last = nc.scalar.activation(prob[:, k, r, :],
                                                        s_ps[h][:, r * ROWS:(r + 1) * ROWS],
                                                        ACT.Exp, bias=neg_max[:, k, r:r + 1],
                                                        accum_out=sums[:, k, r:r + 1])
                        last.then_inc(prob_ready, 1)
                    t = when(s, MIX, 1, STEPS)
                    if h == 0 and t is not None:
                        if t >= 2:
                            act.wait_ge(mixed, t - 1 + turns(16))
                        act.wait_ge(turned, 2 * t + 1 + turns(32))
                        nc.scalar.activation(prob_t[:, slot(t, 2), 0, :, :].rearrange("p a b -> p (a b)"),
                                             pt_ps[0][:, :], ACT.Copy).then_inc(prob_t_ready[0], 1)

                t = when(s, -PROJECT, 1, STEPS)
                if t is not None:
                    if t >= RING:
                        act.wait_ge(scores_made, 2 * (t - RING) + 2 + turns(32))
                    act.wait_ge(projected, t + 1 + turns(16))
                    for h in range(2):
                        rows = slice(h * HALF, (h + 1) * HALF)
                        nc.scalar.activation(stack[rows, slot(t, RING) * 2 + h, 0:2, :]
                                             .rearrange("p a b -> p (a b)"),
                                             qk_ps[rows, :], ACT.Copy).then_inc(hi_ready, 1)

                b = when(s, TURN_X, PAIRS, SEQS)
                if b is not None:
                    if b == 0:
                        act.wait_ge(small_in, 48)
                    if b >= 1:
                        act.wait_ge(h_lo_ready, b + turns(2))
                    act.wait_ge(x_turned, b + 1 + turns(2))
                    for d in range(DT):
                        last = nc.scalar.activation(h_full[:, d, :],
                                                    misc_ps[:, d * ROWS:(d + 1) * ROWS],
                                                    ACT.Identity, bias=beta_c[:, d:d + 1],
                                                    scale=gamma_c[:, d:d + 1])
                    last.then_inc(h_full_ready, 1)

                g = when(s, -2, GROUP, STEPS // GROUP)
                if g is not None:
                    act.wait_ge(v_made, 2 * g + 1 + turns(8))
                    nc.scalar.activation(v_sb[:, slot(g, 2), 0, :], misc_ps[:, :], ACT.Copy)\
                        .then_inc(v_ready[0], 1)

                t = when(s, MIX, 1, STEPS)
                if t is not None:
                    if t >= 2:
                        act.wait_ge(o_added, t - 1 + turns(16))
                    act.wait_ge(mixed, t + 1 + turns(16))
                    nc.scalar.activation(mix_hi[:, slot(t, 2), :], mix_ps[:, 0:ROWS], ACT.Copy)\
                        .then_inc(mix_hi_ready, 1)

            walk(act, step)

        @block.vector
        def _(dve):
            for k in range(2):
                nc.vector.memset(y_sb[:, k, :, :], 0.0).then_inc(y_free[k], 16)

            def weight_lo(i):
                dve.wait_ge(w_hi_ready, i + 1)
                nc.vector.tensor_tensor(w_lo[:, LO_OF[i], :], w_raw[:, i % RAWS, :],
                                        w_hi[:, i, :].bitcast(fp32), ALU.subtract)\
                    .then_inc(w_lo_ready, 1)

            def step(s, turns):
                if s == TURN_X - 2:
                    for i in range(Q0, K0):
                        weight_lo(i)
                if s == TURN_C2 - 1:
                    for i in range(K0, K0 + 2):
                        weight_lo(i)
                if s == TURN_C2 + 1:
                    for i in (V0, V0 + 1, O0, O0 + 1):
                        weight_lo(i)

                t = when(s, 0, 1, STEPS)
                if t is not None:
                    for h in range(2):
                        dve.wait_ge(scores_made, 2 * t + h + 1 + turns(32))
                        nc.vector.tensor_reduce(neg_max[:, slot(t, RING) * 2 + h, :],
                                                s_ps[h][:, :].rearrange("p (r j) -> p r j", r=RT),
                                                AX, ALU.max, negate=True).then_inc(max_ready, 1)
                t = when(s, MIX, 1, STEPS)
                if t is not None:
                    if t >= 2:
                        dve.wait_ge(mixed, t - 1 + turns(16))
                    dve.wait_ge(turned, 2 * t + 2 + turns(32))
                    nc.vector.tensor_copy(prob_t[:, slot(t, 2), 1, :, :].rearrange("p a b -> p (a b)"),
                                          pt_ps[1][:, :]).then_inc(prob_t_ready[1], 1)
                t = when(s, 0, 1, STEPS)
                if t is not None:
                    for h in range(2):
                        k = slot(t, RING) * 2 + h
                        dve.wait_ge(prob_ready, 2 * t + h + 1 + turns(32))
                        nc.vector.reciprocal(inv[:, k, :], sums[:, k, :]).then_inc(inv_ready, 1)

                t = when(s, -PROJECT, 1, STEPS)
                if t is not None:
                    e = slot(t, RING) * 2
                    for h in range(2):
                        rows = slice(h * HALF, (h + 1) * HALF)
                        dve.wait_ge(hi_ready, 2 * t + h + 1 + turns(32))
                        nc.vector.tensor_tensor(stack[rows, e + h, 2, :], qk_ps[rows, ROWS:2 * ROWS],
                                                stack[rows, e + h, 1, :].bitcast(fp32),
                                                ALU.subtract).then_inc(lo_ready, 1)
                    for h in range(2):
                        rows = slice(h * HALF, (h + 1) * HALF)
                        other = slice((1 - h) * HALF, (2 - h) * HALF)
                        nc.vector.tensor_tensor(stack[other, e + h, 0, :], qk_ps[rows, 0:ROWS],
                                                stack[rows, e + h, 0, :].bitcast(fp32),
                                                ALU.subtract).then_inc(lo_ready, 1)

                b = when(s, STATS, PAIRS, SEQS)
                if b is not None:
                    k = slot(b, 2)
                    dve.wait_ge(x_loaded[k], 16 * (b // 2 + 1) + turns(16))
                    if b >= 1:
                        dve.wait_ge(x_norm_ready, b + turns(2))
                    for r in range(RT):
                        last = nc.vector.bn_stats(bn[:, r, :], x_in[:, k, r, :])
                    last.then_inc(stats_done, 1)
                    dve.wait_ge(stats_done, b + 1 + turns(2))
                    nc.vector.memset(var_eps[:, :], 0.0)
                    for r in range(RT):
                        last = nc.vector.bn_aggr(mean_var[:, r, :], bn[:, r, :])
                    last.then_inc(aggr_done, 1)
                    dve.wait_ge(aggr_done, b + 1 + turns(2))
                    nc.vector.tensor_scalar(var_eps[:, :], mean_var[:, :, 1], EPS, None, ALU.add)\
                        .then_inc(var_ready, 1)

                b = when(s, SPLIT_C, PAIRS, SEQS)
                if b is not None:
                    k = slot(b, 2)
                    dve.wait_ge(c_loaded[k], 16 * (b // 2 + 1) + turns(16))
                    if b >= 1:
                        dve.wait_ge(c_turned, 2 * b + turns(4))
                    nc.vector.tensor_copy(c_split[:, :, 0:D_CTX], c_in[:, k, :, :])\
                        .then_inc(c_hi_ready, 1)
                    dve.wait_ge(c_hi_ready, b + 1 + turns(2))
                    nc.vector.tensor_tensor(c_split[:, :, D_CTX:2 * D_CTX], c_in[:, k, :, :],
                                            c_split[:, :, 0:D_CTX].bitcast(fp32), ALU.subtract)\
                        .then_inc(c_split_ready, 1)

                b = when(s, TURN_X, PAIRS, SEQS)
                if b is not None:
                    k = slot(b, 2)
                    if b >= 2:
                        dve.wait_ge(projected, PAIRS * (b - 1) + turns(16))
                    dve.wait_ge(h_full_ready, b + 1 + turns(2))
                    nc.vector.tensor_copy(h_hi[:, k, :, :], h_full[:, :, :]).then_inc(h_hi_ready, 1)
                    dve.wait_ge(h_hi_ready, b + 1 + turns(2))
                    nc.vector.tensor_tensor(h_lo[:, k, :, :], h_full[:, :, :],
                                            h_hi[:, k, :, :].bitcast(fp32), ALU.subtract)\
                        .then_inc(h_lo_ready, 1)

                for part, (offset, tiles) in enumerate(((TURN_C, 2), (TURN_C2, CT - 2))):
                    b = when(s, offset, PAIRS, SEQS)
                    if b is not None:
                        if b >= 2:
                            dve.wait_ge(projected, PAIRS * (b - 1) + turns(16))
                            dve.wait_ge(v_made, 4 * (b - 1) + turns(8))
                        dve.wait_ge(c_turned, 2 * b + part + 1 + turns(4))
                        nc.vector.tensor_copy(c_t[:, slot(b, 2), 2 * part:2 * part + tiles, :]
                                              .rearrange("p a b -> p (a b)"),
                                              misc_ps[:, 0:tiles * ROWS]).then_inc(c_t_ready, 1)

                g = when(s, -1, GROUP, STEPS // GROUP)
                if g is not None:
                    dve.wait_ge(v_made, 2 * g + 2 + turns(8))
                    nc.vector.tensor_copy(v_sb[:, slot(g, 2), 1, :], misc_ps[:, :])\
                        .then_inc(v_ready[1], 1)

                t = when(s, MIX, 1, STEPS)
                if t is not None:
                    dve.wait_ge(mix_hi_ready, t + 1 + turns(16))
                    nc.vector.tensor_tensor(mix_lo[:, slot(t, 2), :], mix_ps[:, 0:ROWS],
                                            mix_hi[:, slot(t, 2), :].bitcast(fp32), ALU.subtract)\
                        .then_inc(mix_lo_ready, 1)

                b = when(s, PUT, PAIRS, SEQS)
                if b is not None:
                    k = slot(b, 2)
                    dve.wait_ge(y_free[k], 16 * (b // 2 + 1) + turns(16))
                    dve.wait_ge(x_bias_ready, b + 1 + turns(2))
                    dve.wait_ge(o_added, PAIRS * (b + 1) + turns(16))
                    nc.vector.tensor_tensor(y_sb[:, k, :, :].rearrange("p a b -> p (a b)"), o_ps[:, :],
                                            x_bias[:, k, :, :].rearrange("p a b -> p (a b)"),
                                            ALU.add).then_inc(y_ready, 1)

            walk(dve, step)

        @block.tensor
        def _(pe):
            def context_products():
                return [(w_hi, k, k) for k in range(CT)] + [(w_lo, k, k) for k in range(2)]

            def step(s, turns):
                t = when(s, 0, 1, STEPS)
                if t is not None:
                    pe.wait_ge(twice[slot(t, RING)], 32 * (t // RING + 1) + turns(128))
                    for h in range(2):
                        k = slot(t, RING) * 2 + h
                        pe.wait_ge(lo_ready, 4 * t + 3 + h + turns(64))
                        if t >= 1:
                            pe.wait_ge(prob_ready, 2 * (t - 1) + h + 1 + turns(32))
                        for r in range(RT):
                            for part in range(2):
                                last = nc.tensor.matmul(
                                    s_ps[h][:, r * ROWS:(r + 1) * ROWS],
                                    stack[:, k, 1 + part, r * P:(r + 1) * P], stack[:, k, 0, :],
                                    start=part == 0, stop=part == 1)
                        last.then_inc(scores_made, 1)

                t = when(s, MIX, 1, STEPS)
                if t is not None:
                    for h in range(2):
                        k = slot(t, RING) * 2 + h
                        pe.wait_ge(scaled, 2 * t + h + 1 + turns(32))
                        if t >= 1:
                            pe.wait_ge(prob_t_ready[h], t + turns(16))
                        for r in range(RT):
                            for j in range(RT):
                                last = nc.tensor.transpose(
                                    pt_ps[h][:, j * ROWS + r * P:j * ROWS + (r + 1) * P],
                                    prob[:, k, r, j * P:(j + 1) * P], ident[:, :])
                        last.then_inc(turned, 1)

                t = when(s, -PROJECT, 1, STEPS)
                if t is not None:
                    b, p = divmod(t, PAIRS)
                    k = slot(b, 2)
                    cols = slice(p * P, (p + 1) * P)
                    if t == 0:
                        pe.wait_ge(w_hi_ready, V0)
                        pe.wait_ge(w_lo_ready, 4)
                    if p == 0:
                        pe.wait_ge(c_t_ready, 2 * b + 2 + turns(4))
                        pe.wait_ge(h_lo_ready, b + 1 + turns(2))
                    if t >= 1:
                        pe.wait_ge(lo_ready, 4 * t + turns(64))
                    passes = context_products()
                    for n, (w, wk, ck) in enumerate(passes):
                        nc.tensor.matmul(qk_ps[:, 0:ROWS], w[:, K0 + wk, cols], c_t[:, k, ck, :],
                                         start=n == 0, stop=n == len(passes) - 1)
                    passes = [(w, d, h) for w, h in ((w_hi, h_hi), (w_hi, h_lo), (w_lo, h_hi))
                              for d in range(DT)]
                    for n, (w, d, h) in enumerate(passes):
                        last = nc.tensor.matmul(qk_ps[:, ROWS:2 * ROWS], w[:, Q0 + d, cols],
                                                h[:, k, d, :], start=n == 0, stop=n == len(passes) - 1)
                    last.then_inc(projected, 1)

                t = when(s, MIX, 1, STEPS)
                if t is not None:
                    g, p = divmod(t, GROUP)
                    if p == 0:
                        for j in range(RT):
                            pe.wait_ge(v_ready[j], g + 1 + turns(4))
                    if t >= 1:
                        pe.wait_ge(mix_lo_ready, t + turns(16))
                    for j in range(RT):
                        for h in range(2):
                            if j == 0:
                                pe.wait_ge(prob_t_ready[h], t + 1 + turns(16))
                            last = nc.tensor.matmul(
                                mix_ps[h * HALF:(h + 1) * HALF, 0:ROWS],
                                v_sb[:, slot(g, 2), j, p * P + h * HALF:p * P + (h + 1) * HALF],
                                prob_t[:, slot(t, 2), h, j, :], start=j == 0, stop=j == RT - 1)
                    last.then_inc(mixed, 1)

                b = when(s, TURN_X, PAIRS, SEQS)
                if b is not None:
                    if b == 0:
                        pe.wait_ge(consts_ready, 1)
                    if b >= 1:
                        pe.wait_ge(v_ready[1], 2 * (b - 1) + 1 + turns(4))
                    pe.wait_ge(x_norm_ready, b + 1 + turns(2))
                    for d in range(DT):
                        for r in range(RT):
                            last = nc.tensor.transpose(
                                misc_ps[:, d * ROWS + r * P:d * ROWS + (r + 1) * P],
                                x_norm[:, r, d * P:(d + 1) * P], ident[:, :])
                    last.then_inc(x_turned, 1)

                for part, (offset, tiles) in enumerate(((TURN_C, 2), (TURN_C2, CT - 2))):
                    b = when(s, offset, PAIRS, SEQS)
                    if b is not None:
                        if part == 0:
                            pe.wait_ge(h_full_ready, b + 1 + turns(2))
                        elif b >= 1:
                            pe.wait_ge(v_ready[1], 2 * b + turns(4))
                        else:
                            pe.wait_ge(c_t_ready, 1)
                        pe.wait_ge(c_split_ready, b + 1 + turns(2))
                        for n in range(tiles):
                            cols = slice((2 * part + n) * P, (2 * part + n + 1) * P)
                            for r in range(RT):
                                last = nc.tensor.transpose(
                                    misc_ps[:, n * ROWS + r * P:n * ROWS + (r + 1) * P],
                                    c_split[:, r, cols].bitcast(fp32), ident[:, :])
                        last.then_inc(c_turned, 1)

                for j in range(RT):
                    g = when(s, j - 2, GROUP, STEPS // GROUP)
                    if g is not None:
                        b, half = divmod(g, 2)
                        if g == 0 and j == 0:
                            pe.wait_ge(w_hi_ready, O0)
                            pe.wait_ge(w_lo_ready, 6)
                        if j == 1:
                            pe.wait_ge(v_ready[0], g + 1 + turns(4))
                        elif half == 0:
                            pe.wait_ge(c_t_ready, 2 * b + 2 + turns(4))
                        elif b + 1 < SEQS:
                            pe.wait_ge(c_t_ready, 2 * b + 3 + turns(4))
                        else:
                            pe.wait_ge(v_ready[1], g)
                        cols = slice(half * GROUP * P, (half + 1) * GROUP * P)
                        passes = context_products()
                        for n, (w, wk, ck) in enumerate(passes):
                            wk = wk + V0 if w is w_hi else LO_OF[V0 + wk]
                            last = nc.tensor.matmul(misc_ps[:, :],
                                                    c_t[:, slot(b, 2), ck, j * P:(j + 1) * P],
                                                    w[:, wk, cols],
                                                    start=n == 0, stop=n == len(passes) - 1)
                        last.then_inc(v_made, 1)

                t = when(s, OUT, 1, STEPS)
                if t is not None:
                    b, p = divmod(t, PAIRS)
                    if t == 0:
                        pe.wait_ge(w_hi_ready, CHUNKS)
                        pe.wait_ge(w_lo_ready, len(LO_OF))
                    if p == 0 and b >= 1:
                        pe.wait_ge(y_ready, b + turns(2))
                    pe.wait_ge(mix_lo_ready, t + 1 + turns(16))
                    o, cols = divmod(p, GROUP)
                    cols = slice(cols * D, (cols + 1) * D)
                    for r in range(RT):
                        passes = [(mix_hi, w_hi, O0 + o), (mix_lo, w_hi, O0 + o),
                                  (mix_hi, w_lo, LO_OF[O0 + o])]
                        for n, (m, w, wk) in enumerate(passes):
                            last = nc.tensor.matmul(o_ps[:, r * D:(r + 1) * D],
                                                    m[:, slot(t, 2), r * P:(r + 1) * P],
                                                    w[:, wk, cols],
                                                    start=p == 0 and n == 0 and r == 0,
                                                    stop=p == PAIRS - 1 and n == 2,
                                                    skip_group_check=True)
                    last.then_inc(o_added, 1)

            walk(pe, step)


_INS = ["x", "ctx_768", "L0_xattn_Wq", "L0_xattn_Wk", "L0_xattn_Wv", "L0_xattn_Wo", "L0_xattn_bo",
        "L0_xattn_gamma", "L0_xattn_beta"]
_OUTS = [((8, 256, 256), "float32")]


def kernel(**inputs):
    import numpy as _np
    import concourse.bacc as _bacc
    from concourse import mybir as _mybir
    from concourse.bass_utils import run_bass_kernel_spmd as _run

    nc = _bacc.Bacc("TRN2", target_bir_lowering=False, num_devices=1)
    arrays, args = {}, []
    for name in _INS:
        a = _np.ascontiguousarray(inputs[name])
        arrays[f"in_{name}_dram"] = a
        args.append(nc.dram_tensor(f"in_{name}_dram", a.shape, _mybir.dt.from_np(a.dtype), kind="ExternalInput").ap())
    for i, (shape, dtype) in enumerate(_OUTS):
        dt = _mybir.dt.from_np(_np.dtype(dtype))
        args.append(nc.dram_tensor(f"out_{i}_dram", shape, dt, kind="ExternalOutput").ap())
    cross_attention_block(nc, *args)
    r = _run(nc, [arrays], core_ids=[0])
    return r.results[0]["out_0_dram"]
```

```python
import concourse.bass as bass
from concourse import mybir
from contextlib import ExitStack


def cross_attention_block(nc, x, ctx_in, w_q, w_k, w_v, w_o, b_o, gamma, beta, out):
    fp32 = mybir.dt.float32
    fp32r = mybir.dt.float32r
    ALU = mybir.AluOpType
    ACT = mybir.ActivationFunctionType
    AX = mybir.AxisListType.X

    P = 128
    SEQS, ROWS, D = x.shape
    D_CTX = ctx_in.shape[2]
    INNER = w_q.shape[1]
    HEAD = 64
    HALF = P // 2
    PAIRS = INNER // P
    STEPS = SEQS * PAIRS
    RT = ROWS // P
    DT = D // P
    EPS = 1e-5
    SCALE = HEAD ** -0.5
    GROUP = 4
    RING = 4
    PROJECT, MIX, OUT = 2, 2, 3
    LOOP_FROM, LOOP_STEPS, LOOPS = 4, 2 * PAIRS, 3
    FIRST, LAST = -11, STEPS + OUT + 1

    CT = 2 * D_CTX // P
    CREST = D_CTX - P

    x_v = x.rearrange("b (r p) d -> b p r d", p=P)
    c_v = ctx_in.rearrange("b (r p) d -> b p r d", p=P)
    y_v = out.rearrange("b (r p) d -> b p r d", p=P)

    Q0, K0, V0, O0, TILES = 0, 2, 5, 8, 10
    LO_OF = {0: 0, 1: 1, 2: 2, 3: 3, 5: 4, 6: 5, 8: 6, 9: 7}
    PIECE = INNER // 2
    PIECES = [(i, half) for half in range(2) for i in range(O0)]
    PIECES += [(i, half) for i in range(O0, TILES) for half in range(2)]
    WARM = 6
    RAWS = 10
    HI_SCALAR = {-10: (0, 1, 2), -9: (3,), -7: (4,), -5: (5, 6, 7), -3: (8, 9),
                 -1: (10, 11, 12, 13), 0: (14, 15), 2: (16, 17), 3: (18, 19)}
    LO_VECTOR = {-9: (2, 3), -5: (5, 6)}
    LO_POOL = {-10: (0, 1), -3: (8, 9), -1: (10, 11), 0: (13, 14), 1: (16, 17), 3: (18, 19)}
    LOAD_LATE = {-3: (10, 11, 12, 13, 14), -2: (15, 16, 17), 1: (18, 19)}

    with ExitStack() as ctx:
        def sb(name, shape, dt=fp32):
            return ctx.enter_context(nc.sbuf_tensor(name, shape, dt))

        def bank(name):
            return ctx.enter_context(nc.psum_tensor(name, [P, 512], fp32))

        def sem(name):
            return ctx.enter_context(nc.semaphore(name))

        w_raw = sb("w_raw", [P, RAWS, PIECE])
        w_hi = sb("w_hi", [P, TILES, INNER], fp32r)
        w_lo = sb("w_lo", [P, len(LO_OF), INNER], fp32r)
        ident = sb("ident", [P, P])
        gamma_c = sb("gamma_c", [P, DT])
        beta_c = sb("beta_c", [P, DT])
        bo_b = sb("bo_b", [P, D])
        neg_half = sb("neg_half", [P, RT])
        x_in = sb("x_in", [P, 2, RT, D])
        c_in = sb("c_in", [P, 2, RT, D_CTX])
        bn = sb("bn", [P, RT, 6])
        mean_var = sb("mean_var", [P, RT, 2])
        var_eps = sb("var_eps", [P, RT])
        rstd = sb("rstd", [P, RT])
        x_norm = sb("x_norm", [P, RT, D])
        x_bias = sb("x_bias", [P, 2, RT, D])
        c_split = sb("c_split", [P, RT, 2 * D_CTX], fp32r)
        h_full = sb("h_full", [P, DT, ROWS])
        h_hi = sb("h_hi", [P, 2, DT, ROWS], fp32r)
        h_lo = sb("h_lo", [P, 2, DT, ROWS], fp32r)
        c_t = sb("c_t", [P, 2, CT, ROWS], fp32r)
        stack = sb("stack", [P, RING * 2, 3, ROWS], fp32r)
        v_sb = sb("v_sb", [P, 2, RT, GROUP * P])
        neg_max = sb("neg_max", [P, RING * 2, RT])
        sums = sb("sums", [P, RING * 2, RT])
        inv = sb("inv", [P, RING * 2, RT])
        prob = sb("prob", [P, RING * 2, RT, ROWS])
        prob_t = sb("prob_t", [P, 2, 2, RT, ROWS])
        mix_hi = sb("mix_hi", [P, 2, ROWS], fp32r)
        mix_lo = sb("mix_lo", [P, 2, ROWS], fp32r)
        y_sb = sb("y_sb", [P, 2, RT, D])

        qk_ps = bank("qk_ps")
        misc_ps = bank("misc_ps")
        s_ps = [bank("s_even_ps"), bank("s_odd_ps")]
        pt_ps = [bank("pt_even_ps"), bank("pt_odd_ps")]
        mix_ps = bank("mix_ps")
        o_ps = bank("o_ps")

        w_in = [sem(f"w_in{i}") for i in range(len(PIECES))]
        x_loaded = [sem("x_loaded0"), sem("x_loaded1")]
        c_loaded = [sem("c_loaded0"), sem("c_loaded1")]
        small_in = sem("small_in")
        ident_zero = sem("ident_zero")
        consts_ready = sem("consts_ready")
        w_hi_ready = sem("w_hi_ready")
        w_lo_ready = sem("w_lo_ready")
        w_lo_pool_ready = sem("w_lo_pool_ready")
        stats_done = sem("stats_done")
        aggr_done = sem("aggr_done")
        var_ready = sem("var_ready")
        rstd_ready = sem("rstd_ready")
        x_norm_ready = sem("x_norm_ready")
        x_bias_ready = sem("x_bias_ready")
        c_hi_ready = sem("c_hi_ready")
        c_split_ready = sem("c_split_ready")
        x_turned = sem("x_turned")
        c_turned = sem("c_turned")
        h_full_ready = sem("h_full_ready")
        h_hi_ready = sem("h_hi_ready")
        h_lo_ready = sem("h_lo_ready")
        c_t_ready = sem("c_t_ready")
        projected = sem("projected")
        hi_ready = sem("hi_ready")
        lo_ready = sem("lo_ready")
        twice = [sem(f"twice{i}") for i in range(RING)]
        v_made = sem("v_made")
        v_ready = [sem("v_ready0"), sem("v_ready1")]
        scores_made = sem("scores_made")
        max_ready = sem("max_ready")
        prob_ready = sem("prob_ready")
        inv_ready = sem("inv_ready")
        scaled = sem("scaled")
        turned = sem("turned")
        prob_t_ready = [sem("prob_t_ready_even"), sem("prob_t_ready_odd")]
        mixed = sem("mixed")
        mix_hi_ready = sem("mix_hi_ready")
        mix_lo_ready = sem("mix_lo_ready")
        o_added = sem("o_added")
        y_ready = sem("y_ready")
        y_free = [sem("y_free0"), sem("y_free1")]

        block = ctx.enter_context(nc.Block())

        def when(s, offset, every, count):
            n, rest = divmod(s - offset, every)
            return n if rest == 0 and 0 <= n < count else None

        def slot(n, ring):
            return n % ring

        def walk(engine, step):
            for s in range(FIRST, LOOP_FROM):
                step(s, lambda n: 0)
            with engine.Fori(0, LOOPS) as turn:
                for s in range(LOOP_FROM, LOOP_FROM + LOOP_STEPS):
                    step(s, lambda n: turn * n)
            for s in range(LOOP_FROM + LOOP_STEPS * LOOPS, LAST):
                step(s, lambda n: 0)

        def through(tile, half):
            return PIECES.index((tile, half)) + 1

        def before(n, pieces):
            return sum(1 for step in pieces.values() for piece in step if piece < n)

        def weights_ready(engine, n):
            engine.wait_ge(w_hi_ready, n)
            if before(n, LO_VECTOR):
                engine.wait_ge(w_lo_ready, before(n, LO_VECTOR))
            if before(n, LO_POOL):
                engine.wait_ge(w_lo_pool_ready, before(n, LO_POOL))

        LOAD, STATS, SPLIT_C, TURN_X, TURN_C, BIAS_X, TURN_C2 = -12, -11, -10, -8, -7, -5, -4
        PUT = PAIRS - 1 + OUT

        @block.sync
        def _(sp):
            def load_weight(n):
                if n >= RAWS:
                    weights_ready(sp, n - RAWS + 1)
                i, half = PIECES[n]
                dst = w_raw[:, n % RAWS, :]
                cols = slice(half * PIECE, (half + 1) * PIECE)
                if i < K0:
                    sp.dma_start(dst, w_q[i * P:(i + 1) * P, cols]).then_inc(w_in[n], 16)
                elif i < O0:
                    w, k = (w_k, i - K0) if i < V0 else (w_v, i - V0)
                    if k == 0:
                        sp.dma_start(dst, w[0:P, cols]).then_inc(w_in[n], 16)
                    elif k == 1:
                        sp.dma_start(dst[0:CREST, :], w[P:D_CTX, cols]).then_inc(w_in[n], 16)
                        sp.dma_start(dst[CREST:P, :], w[0:P - CREST, cols]).then_inc(w_in[n], 16)
                    else:
                        sp.dma_start(dst, w[D_CTX - P:D_CTX, cols]).then_inc(w_in[n], 16)
                else:
                    first = ((i - O0) * GROUP + half * GROUP // 2) * P
                    rows = w_o[first:first + GROUP // 2 * P, :]
                    sp.dma_start(dst.rearrange("p (g n) -> p g n", g=GROUP // 2),
                                 rows.rearrange("(g p) n -> p g n", p=P)).then_inc(w_in[n], 16)

            def load_x(b, sequence):
                k = slot(b, 2)
                sp.dma_start(x_in[:, k, :, :], x_v[sequence]).then_inc(x_loaded[k], 16)

            def load_c(b, sequence):
                k = slot(b, 2)
                sp.dma_start(c_in[:, k, :, :], c_v[sequence]).then_inc(c_loaded[k], 16)

            def number(n):
                return n if isinstance(n, int) else sp.snap(n)

            load_x(0, 0)
            load_c(0, 0)
            load_weight(0)
            load_weight(1)
            for n in range(K0, V0):
                load_weight(n)
            for n in range(V0, O0):
                load_weight(n)
            load_x(1, 1)
            load_c(1, 1)
            for n in range(O0, RAWS):
                load_weight(n)

            def step(s, turns):
                for n in LOAD_LATE.get(s, ()) if s < -2 else ():
                    load_weight(n)
                b = when(s, LOAD, PAIRS, SEQS)
                if b is not None and b >= 2:
                    sequence, used = number(b + turns(2)), number(b - 1 + turns(2))
                    sp.wait_ge(x_norm_ready, used)
                    sp.wait_ge(x_bias_ready, used)
                    sp.wait_ge(c_split_ready, used)
                    load_x(b, sequence)
                    load_c(b, sequence)
                t = when(s, -PROJECT, 1, STEPS)
                if t is not None:
                    for h in range(2):
                        k = slot(t, RING) * 2 + h
                        own = slice(h * HALF, (h + 1) * HALF)
                        other = slice((1 - h) * HALF, (2 - h) * HALF)
                        split = number(4 * t + 1 + h + turns(64))
                        sp.wait_ge(lo_ready, split)
                        sp.dma_start(stack[other, k, 1:3, :].bitcast(fp32),
                                     stack[own, k, 1:3, :].bitcast(fp32))\
                            .then_inc(twice[slot(t, RING)], 16)
                for n in LOAD_LATE.get(s, ()) if s >= -2 else ():
                    load_weight(n)
                b = when(s, PUT + 1, PAIRS, SEQS)
                if b is not None:
                    sequence, added = number(b + turns(2)), number(b + 1 + turns(2))
                    sp.wait_ge(y_ready, added)
                    sp.dma_start(y_v[sequence], y_sb[:, slot(b, 2), :, :])\
                        .then_inc(y_free[slot(b, 2)], 16)

            walk(sp, step)
            for k in range(2):
                sp.wait_ge(y_free[k], 16 * (SEQS // 2 + 1))

        @block.gpsimd
        def _(pool):
            pool.dma_start(gamma_c[:, :], gamma.rearrange("(t p) -> p t", p=P),
                           allow_slow_non_contiguous=True).then_inc(small_in, 16)
            pool.dma_start(beta_c[:, :], beta.rearrange("(t p) -> p t", p=P),
                           allow_slow_non_contiguous=True).then_inc(small_in, 16)
            pool.dma_start(bo_b[:, :], b_o.partition_broadcast(P)).then_inc(small_in, 16)
            nc.gpsimd.memset(ident[:, :], 0.0).then_inc(ident_zero, 1)
            nc.gpsimd.memset(neg_half[:, :], -0.5).then_inc(ident_zero, 1)
            pool.wait_ge(ident_zero, 2)
            nc.gpsimd.affine_select(out=ident[:, :], in_=ident[:, :], compare_op=ALU.not_equal,
                                    fill=1.0, base=0, pattern=[[-1, P]], channel_multiplier=1)\
                .then_inc(consts_ready, 1)

            def step(s, turns):
                b = when(s, STATS, PAIRS, SEQS)
                if b is not None:
                    pool.wait_ge(var_ready, b + 1 + turns(2))
                    nc.gpsimd.tensor_tensor(rstd[:, :], var_eps[:, :], neg_half[:, :], ALU.pow)\
                        .then_inc(rstd_ready, 1)
                t = when(s, 0, 1, STEPS)
                if t is not None:
                    for h in range(2):
                        k = slot(t, RING) * 2 + h
                        pool.wait_ge(inv_ready, 2 * t + h + 1 + turns(32))
                        for r in range(RT):
                            last = nc.gpsimd.tensor_scalar(prob[:, k, r, :], prob[:, k, r, :],
                                                           inv[:, k, r:r + 1], SCALE,
                                                           ALU.mult, ALU.mult)
                        last.then_inc(scaled, 1)
                for n in LO_POOL.get(s, ()):
                    i, half = PIECES[n]
                    cols = slice(half * PIECE, (half + 1) * PIECE)
                    pool.wait_ge(w_hi_ready, n + 1)
                    nc.gpsimd.tensor_tensor(w_lo[:, LO_OF[i], cols], w_raw[:, n % RAWS, :],
                                            w_hi[:, i, cols].bitcast(fp32), ALU.subtract)\
                        .then_inc(w_lo_pool_ready, 1)
                b = when(s, SPLIT_C, PAIRS, SEQS)
                if b is not None and b > 0:
                    pool.wait_ge(c_hi_ready, b + 1 + turns(2))
                    for r in range(RT):
                        last = nc.gpsimd.tensor_tensor(c_split[:, r, D_CTX:2 * D_CTX],
                                                       c_in[:, slot(b, 2), r, :],
                                                       c_split[:, r, 0:D_CTX].bitcast(fp32),
                                                       ALU.subtract)
                    last.then_inc(c_split_ready, 1)
                b = when(s, TURN_X + 1, PAIRS, SEQS)
                if b is not None and b > 0:
                    pool.wait_ge(h_hi_ready, b + 1 + turns(2))
                    for d in range(DT):
                        last = nc.gpsimd.tensor_tensor(h_lo[:, slot(b, 2), d, :], h_full[:, d, :],
                                                       h_hi[:, slot(b, 2), d, :].bitcast(fp32),
                                                       ALU.subtract)
                    last.then_inc(h_lo_ready, 1)
                b = when(s, BIAS_X, PAIRS, SEQS)
                if b is not None:
                    if b == 0:
                        pool.wait_ge(small_in, 48)
                    if b >= 2:
                        pool.wait_ge(y_ready, b - 1 + turns(2))
                    for r in range(RT):
                        last = nc.gpsimd.tensor_tensor(x_bias[:, slot(b, 2), r, :],
                                                       x_in[:, slot(b, 2), r, :], bo_b[:, :],
                                                       ALU.add)
                    last.then_inc(x_bias_ready, 1)

            for s in range(FIRST, LAST):
                step(s, lambda n: 0)

        @block.scalar
        def _(act):
            def weight_hi(n):
                i, half = PIECES[n]
                act.wait_ge(w_in[n], 32 if i in (K0 + 1, V0 + 1) else 16)
                nc.scalar.activation(w_hi[:, i, half * PIECE:(half + 1) * PIECE],
                                     w_raw[:, n % RAWS, :], ACT.Copy).then_inc(w_hi_ready, 1)

            def step(s, turns):
                t = when(s, OUT, 1, STEPS)
                if t is not None:
                    act.wait_ge(mixed, t + 1 + turns(16))
                    nc.scalar.activation(mix_hi[:, slot(t, 2), :], mix_ps[:, 0:ROWS], ACT.Copy)\
                        .then_inc(mix_hi_ready, 1)

                b = when(s, TURN_X + 1, PAIRS, SEQS)
                if b is not None:
                    if b == 0:
                        act.wait_ge(small_in, 48)
                    if b >= 1:
                        act.wait_ge(h_lo_ready, b + turns(2))
                    act.wait_ge(x_turned, b + 1 + turns(2))
                    for d in range(DT):
                        last = nc.scalar.activation(h_full[:, d, :],
                                                    misc_ps[:, d * ROWS:(d + 1) * ROWS],
                                                    ACT.Identity, bias=beta_c[:, d:d + 1],
                                                    scale=gamma_c[:, d:d + 1])
                    last.then_inc(h_full_ready, 1)
                g = when(s, -1, GROUP, STEPS // GROUP)
                if g is not None:
                    act.wait_ge(v_made, 2 * g + 1 + turns(8))
                    nc.scalar.activation(v_sb[:, slot(g, 2), 0, :], misc_ps[:, :], ACT.Copy)\
                        .then_inc(v_ready[0], 1)

                if s == TURN_C:
                    act.wait_ge(c_turned, 1)
                    nc.scalar.activation(c_t[:, 0, 0:2, :].rearrange("p a b -> p (a b)"),
                                         pt_ps[0][:, :], ACT.Copy).then_inc(c_t_ready, 1)

                def probabilities(h):
                    t = when(s, 0, 1, STEPS)
                    if t is not None:
                        k = slot(t, RING) * 2 + h
                        if t >= RING:
                            act.wait_ge(turned, 2 * (t - RING) + h + 1 + turns(32))
                        act.wait_ge(max_ready, 2 * t + h + 1 + turns(32))
                        for r in range(RT):
                            last = nc.scalar.activation(prob[:, k, r, :],
                                                        s_ps[h][:, r * ROWS:(r + 1) * ROWS],
                                                        ACT.Exp, bias=neg_max[:, k, r:r + 1],
                                                        accum_out=sums[:, k, r:r + 1])
                        last.then_inc(prob_ready, 1)

                probabilities(0)

                t = when(s, MIX, 1, STEPS)
                if t is not None:
                    if t >= 2:
                        act.wait_ge(mixed, t - 1 + turns(16))
                    act.wait_ge(turned, 2 * t + 1 + turns(32))
                    nc.scalar.activation(prob_t[:, slot(t, 2), 0, :, :].rearrange("p a b -> p (a b)"),
                                         pt_ps[0][:, :], ACT.Copy).then_inc(prob_t_ready[0], 1)

                t = when(s, -PROJECT, 1, STEPS)
                if t is not None:
                    if t >= RING:
                        act.wait_ge(scores_made, 2 * (t - RING) + 2 + turns(32))
                    act.wait_ge(projected, t + 1 + turns(16))
                    for h in range(2):
                        rows = slice(h * HALF, (h + 1) * HALF)
                        nc.scalar.activation(stack[rows, slot(t, RING) * 2 + h, 0:2, :]
                                             .rearrange("p a b -> p (a b)"),
                                             qk_ps[rows, :], ACT.Copy).then_inc(hi_ready, 1)

                if s == -1:
                    act.wait_ge(v_made, 2)
                    nc.scalar.activation(v_sb[:, 0, 1, :], misc_ps[:, :], ACT.Copy)\
                        .then_inc(v_ready[1], 1)

                probabilities(1)

                for n in HI_SCALAR.get(s, ()):
                    weight_hi(n)

            walk(act, step)

        @block.vector
        def _(dve):
            for k in range(2):
                nc.vector.memset(y_sb[:, k, :, :], 0.0).then_inc(y_free[k], 16)

            def weight_lo(n):
                i, half = PIECES[n]
                cols = slice(half * PIECE, (half + 1) * PIECE)
                dve.wait_ge(w_hi_ready, n + 1)
                nc.vector.tensor_tensor(w_lo[:, LO_OF[i], cols], w_raw[:, n % RAWS, :],
                                        w_hi[:, i, cols].bitcast(fp32), ALU.subtract)\
                    .then_inc(w_lo_ready, 1)

            def step(s, turns):
                t = when(s, 0, 1, STEPS)
                if t is not None:
                    for h in range(2):
                        dve.wait_ge(scores_made, 2 * t + h + 1 + turns(32))
                        nc.vector.tensor_reduce(neg_max[:, slot(t, RING) * 2 + h, :],
                                                s_ps[h][:, :].rearrange("p (r j) -> p r j", r=RT),
                                                AX, ALU.max, negate=True).then_inc(max_ready, 1)

                t = when(s, OUT, 1, STEPS)
                if t is not None:
                    dve.wait_ge(mix_hi_ready, t + 1 + turns(16))
                    nc.vector.tensor_tensor(mix_lo[:, slot(t, 2), :], mix_ps[:, 0:ROWS],
                                            mix_hi[:, slot(t, 2), :].bitcast(fp32), ALU.subtract)\
                        .then_inc(mix_lo_ready, 1)

                t = when(s, 1, 1, STEPS)
                if t is not None:
                    for h in range(2):
                        k = slot(t, RING) * 2 + h
                        dve.wait_ge(prob_ready, 2 * t + h + 1 + turns(32))
                        nc.vector.reciprocal(inv[:, k, :], sums[:, k, :]).then_inc(inv_ready, 1)

                b = when(s, PUT + 1, PAIRS, SEQS)
                if b is not None:
                    k = slot(b, 2)
                    dve.wait_ge(y_free[k], 16 * (b // 2 + 1) + turns(16))
                    dve.wait_ge(x_bias_ready, b + 1 + turns(2))
                    dve.wait_ge(o_added, PAIRS * (b + 1) + turns(16))
                    nc.vector.tensor_tensor(y_sb[:, k, :, :].rearrange("p a b -> p (a b)"), o_ps[:, :],
                                            x_bias[:, k, :, :].rearrange("p a b -> p (a b)"),
                                            ALU.add).then_inc(y_ready, 1)

                for part, (offset, tiles) in enumerate(((TURN_C, 2), (TURN_C2, CT - 2))):
                    b = when(s, offset + 1, PAIRS, SEQS)
                    if s == TURN_C and part == 1:
                        dve.wait_ge(c_turned, 2)
                        nc.vector.tensor_copy(c_t[:, 0, 2:CT, :].rearrange("p a b -> p (a b)"),
                                              pt_ps[1][:, 0:(CT - 2) * ROWS]).then_inc(c_t_ready, 1)
                    if b is not None and b > 0:
                        dve.wait_ge(c_turned, 2 * b + part + 1 + turns(4))
                        nc.vector.tensor_copy(c_t[:, slot(b, 2), 2 * part:2 * part + tiles, :]
                                              .rearrange("p a b -> p (a b)"),
                                              misc_ps[:, 0:tiles * ROWS]).then_inc(c_t_ready, 1)
                g = when(s, 0, GROUP, STEPS // GROUP)
                if g is not None and g > 0:
                    dve.wait_ge(v_made, 2 * g + 2 + turns(8))
                    nc.vector.tensor_copy(v_sb[:, slot(g, 2), 1, :], misc_ps[:, :])\
                        .then_inc(v_ready[1], 1)

                t = when(s, MIX, 1, STEPS)
                if t is not None:
                    if t >= 2:
                        dve.wait_ge(mixed, t - 1 + turns(16))
                    dve.wait_ge(turned, 2 * t + 2 + turns(32))
                    nc.vector.tensor_copy(prob_t[:, slot(t, 2), 1, :, :].rearrange("p a b -> p (a b)"),
                                          pt_ps[1][:, :]).then_inc(prob_t_ready[1], 1)

                def q_lo(h):
                    t = when(s, -PROJECT, 1, STEPS)
                    if t is not None:
                        k = slot(t, RING) * 2 + h
                        rows = slice(h * HALF, (h + 1) * HALF)
                        dve.wait_ge(hi_ready, 2 * t + h + 1 + turns(32))
                        nc.vector.tensor_tensor(stack[rows, k, 2, :], qk_ps[rows, ROWS:2 * ROWS],
                                                stack[rows, k, 1, :].bitcast(fp32),
                                                ALU.subtract).then_inc(lo_ready, 1)

                q_lo(0)
                q_lo(1)
                t = when(s, -PROJECT, 1, STEPS)
                if t is not None:
                    for h in range(2):
                        k = slot(t, RING) * 2 + h
                        rows = slice(h * HALF, (h + 1) * HALF)
                        other = slice((1 - h) * HALF, (2 - h) * HALF)
                        nc.vector.tensor_tensor(stack[other, k, 0, :], qk_ps[rows, 0:ROWS],
                                                stack[rows, k, 0, :].bitcast(fp32),
                                                ALU.subtract).then_inc(lo_ready, 1)

                b = when(s, TURN_X + 1, PAIRS, SEQS)
                if b is not None:
                    dve.wait_ge(h_full_ready, b + 1 + turns(2))
                    nc.vector.tensor_copy(h_hi[:, slot(b, 2), :, :], h_full[:, :, :])\
                        .then_inc(h_hi_ready, 1)
                    if b == 0:
                        dve.wait_ge(h_hi_ready, 1)
                        nc.vector.tensor_tensor(h_lo[:, 0, :, :], h_full[:, :, :],
                                                h_hi[:, 0, :, :].bitcast(fp32),
                                                ALU.subtract).then_inc(h_lo_ready, 1)

                b = when(s, STATS, PAIRS, SEQS)
                if b is not None:
                    k = slot(b, 2)
                    dve.wait_ge(x_loaded[k], 16 * (b // 2 + 1) + turns(16))
                    for r in range(RT):
                        last = nc.vector.bn_stats(bn[:, r, :], x_in[:, k, r, :])
                    last.then_inc(stats_done, 1)
                    dve.wait_ge(stats_done, b + 1 + turns(2))
                    nc.vector.memset(var_eps[:, :], 0.0)
                    for r in range(RT):
                        last = nc.vector.bn_aggr(mean_var[:, r, :], bn[:, r, :])
                    last.then_inc(aggr_done, 1)
                    dve.wait_ge(aggr_done, b + 1 + turns(2))
                    nc.vector.tensor_scalar(var_eps[:, :], mean_var[:, :, 1], EPS, None, ALU.add)\
                        .then_inc(var_ready, 1)

                b = when(s, STATS + 1, PAIRS, SEQS)
                if b is not None:
                    if b >= 1:
                        dve.wait_ge(x_turned, b + turns(2))
                    dve.wait_ge(rstd_ready, b + 1 + turns(2))
                    for r in range(RT):
                        last = nc.vector.tensor_scalar(x_norm[:, r, :], x_in[:, slot(b, 2), r, :],
                                                       mean_var[:, r, 0:1], rstd[:, r:r + 1],
                                                       ALU.subtract, ALU.mult)
                    last.then_inc(x_norm_ready, 1)

                b = 0 if s == FIRST else when(s, SPLIT_C, PAIRS, SEQS)
                if b is not None and (b > 0 or s == FIRST):
                    dve.wait_ge(c_loaded[slot(b, 2)], 16 * (b // 2 + 1) + turns(16))
                    if b >= 1:
                        dve.wait_ge(c_turned, 2 * b + turns(4))
                    nc.vector.tensor_copy(c_split[:, :, 0:D_CTX], c_in[:, slot(b, 2), :, :])\
                        .then_inc(c_hi_ready, 1)
                    if b == 0:
                        dve.wait_ge(c_hi_ready, 1)
                        nc.vector.tensor_tensor(c_split[:, :, D_CTX:2 * D_CTX], c_in[:, 0, :, :],
                                                c_split[:, :, 0:D_CTX].bitcast(fp32),
                                                ALU.subtract).then_inc(c_split_ready, 1)

                for n in LO_VECTOR.get(s, ()):
                    weight_lo(n)

            walk(dve, step)

        @block.tensor
        def _(pe):
            def context_products():
                return [(w_hi, k, k) for k in range(CT)] + [(w_lo, k, k) for k in range(2)]

            def step(s, turns):
                t = when(s, 0, 1, STEPS)
                if t is not None:
                    pe.wait_ge(twice[slot(t, RING)], 32 * (t // RING + 1) + turns(128))
                    for h in range(2):
                        k = slot(t, RING) * 2 + h
                        pe.wait_ge(lo_ready, 4 * t + 3 + h + turns(64))
                        if t >= 1:
                            pe.wait_ge(prob_ready, 2 * (t - 1) + h + 1 + turns(32))
                        for r in range(RT):
                            for part in range(2):
                                last = nc.tensor.matmul(
                                    s_ps[h][:, r * ROWS:(r + 1) * ROWS],
                                    stack[:, k, 1 + part, r * P:(r + 1) * P], stack[:, k, 0, :],
                                    start=part == 0, stop=part == 1)
                        last.then_inc(scores_made, 1)

                t = when(s, -PROJECT, 1, STEPS)
                if t is not None:
                    b, p = divmod(t, PAIRS)
                    k = slot(b, 2)
                    cols = slice(p * P, (p + 1) * P)
                    if t in (0, GROUP):
                        weights_ready(pe, through(V0 - 1, t // GROUP))
                    if p == 0:
                        pe.wait_ge(c_t_ready, 2 * b + 2 + turns(4))
                    if t >= 1:
                        pe.wait_ge(lo_ready, 4 * t + turns(64))
                    passes = context_products()
                    for n, (w, wk, ck) in enumerate(passes):
                        nc.tensor.matmul(qk_ps[:, 0:ROWS], w[:, K0 + wk, cols], c_t[:, k, ck, :],
                                         start=n == 0, stop=n == len(passes) - 1)
                    if p == 0:
                        pe.wait_ge(h_lo_ready, b + 1 + turns(2))
                    passes = [(w, d, h) for w, h in ((w_hi, h_hi), (w_hi, h_lo), (w_lo, h_hi))
                              for d in range(DT)]
                    for n, (w, d, h) in enumerate(passes):
                        last = nc.tensor.matmul(qk_ps[:, ROWS:2 * ROWS], w[:, Q0 + d, cols],
                                                h[:, k, d, :], start=n == 0, stop=n == len(passes) - 1)
                    last.then_inc(projected, 1)

                t = when(s, MIX, 1, STEPS)
                if t is not None:
                    for h in range(2):
                        k = slot(t, RING) * 2 + h
                        pe.wait_ge(scaled, 2 * t + h + 1 + turns(32))
                        if t >= 1:
                            pe.wait_ge(prob_t_ready[h], t + turns(16))
                        for r in range(RT):
                            for j in range(RT):
                                last = nc.tensor.transpose(
                                    pt_ps[h][:, j * ROWS + r * P:j * ROWS + (r + 1) * P],
                                    prob[:, k, r, j * P:(j + 1) * P], ident[:, :])
                        last.then_inc(turned, 1)

                t = when(s, OUT, 1, STEPS)
                if t is not None:
                    b, p = divmod(t, PAIRS)
                    if t in (0, GROUP):
                        weights_ready(pe, through(O0 + t // GROUP, 1))
                    if p == 0 and b >= 1:
                        pe.wait_ge(y_ready, b + turns(2))
                    pe.wait_ge(mix_lo_ready, t + 1 + turns(16))
                    o, cols = divmod(p, GROUP)
                    cols = slice(cols * D, (cols + 1) * D)
                    for r in range(RT):
                        passes = [(mix_hi, w_hi, O0 + o), (mix_lo, w_hi, O0 + o),
                                  (mix_hi, w_lo, LO_OF[O0 + o])]
                        for n, (m, w, wk) in enumerate(passes):
                            last = nc.tensor.matmul(o_ps[:, r * D:(r + 1) * D],
                                                    m[:, slot(t, 2), r * P:(r + 1) * P],
                                                    w[:, wk, cols],
                                                    start=p == 0 and n == 0 and r == 0,
                                                    stop=p == PAIRS - 1 and n == 2,
                                                    skip_group_check=True)
                    last.then_inc(o_added, 1)

                b = when(s, TURN_X, PAIRS, SEQS)
                if b is not None:
                    if b >= 1:
                        pe.wait_ge(v_ready[1], 2 * (b - 1) + 1 + turns(4))
                    pe.wait_ge(x_norm_ready, b + 1 + turns(2))
                    for d in range(DT):
                        for r in range(RT):
                            last = nc.tensor.transpose(
                                misc_ps[:, d * ROWS + r * P:d * ROWS + (r + 1) * P],
                                x_norm[:, r, d * P:(d + 1) * P], ident[:, :])
                    last.then_inc(x_turned, 1)

                for part, (offset, tiles) in enumerate(((TURN_C, 2), (TURN_C2, CT - 2))):
                    b = 0 if s == TURN_C else when(s, offset, PAIRS, SEQS)
                    if b is not None and (b > 0 or s == TURN_C):
                        bank_ps = misc_ps if b > 0 else pt_ps[part]
                        if b == 0:
                            pass
                        elif part == 0:
                            pe.wait_ge(h_full_ready, b + 1 + turns(2))
                        else:
                            pe.wait_ge(v_ready[1], 2 * b + turns(4))
                        pe.wait_ge(c_split_ready, b + 1 + turns(2))
                        for n in range(tiles):
                            cols = slice((2 * part + n) * P, (2 * part + n + 1) * P)
                            for r in range(RT):
                                last = nc.tensor.transpose(
                                    bank_ps[:, n * ROWS + r * P:n * ROWS + (r + 1) * P],
                                    c_split[:, r, cols].bitcast(fp32), ident[:, :])
                        last.then_inc(c_turned, 1)

                for j in range(RT):
                    g = when(s, j - 2, GROUP, STEPS // GROUP)
                    if g is not None:
                        b, half = divmod(g, 2)
                        if s in (-2, GROUP - 2):
                            weights_ready(pe, through(O0 - 1, g))
                        if j == 1:
                            pe.wait_ge(v_ready[0], g + 1 + turns(4))
                        elif half == 0:
                            pe.wait_ge(c_t_ready, 2 * b + 2 + turns(4))
                        elif b + 1 < SEQS:
                            pe.wait_ge(c_t_ready, 2 * b + 3 + turns(4))
                        else:
                            pe.wait_ge(v_ready[1], g)
                        cols = slice(half * GROUP * P, (half + 1) * GROUP * P)
                        passes = context_products()
                        for n, (w, wk, ck) in enumerate(passes):
                            wk = wk + V0 if w is w_hi else LO_OF[V0 + wk]
                            last = nc.tensor.matmul(misc_ps[:, :],
                                                    c_t[:, slot(b, 2), ck, j * P:(j + 1) * P],
                                                    w[:, wk, cols],
                                                    start=n == 0, stop=n == len(passes) - 1)
                        last.then_inc(v_made, 1)

                t = when(s, MIX, 1, STEPS)
                if t is not None:
                    g, p = divmod(t, GROUP)
                    if p == 0:
                        for j in range(RT):
                            pe.wait_ge(v_ready[j], g + 1 + turns(4))
                    if t >= 1:
                        pe.wait_ge(mix_lo_ready, t + turns(16))
                    for j in range(RT):
                        for h in range(2):
                            if j == 0:
                                pe.wait_ge(prob_t_ready[h], t + 1 + turns(16))
                            last = nc.tensor.matmul(
                                mix_ps[h * HALF:(h + 1) * HALF, 0:ROWS],
                                v_sb[:, slot(g, 2), j, p * P + h * HALF:p * P + (h + 1) * HALF],
                                prob_t[:, slot(t, 2), h, j, :], start=j == 0, stop=j == RT - 1)
                    last.then_inc(mixed, 1)

            pe.wait_ge(consts_ready, 1)
            for _ in range(WARM):
                nc.tensor.transpose(o_ps[:, 0:P], ident[:, :], ident[:, :])
            walk(pe, step)


_INS = ["x", "ctx_768", "L0_xattn_Wq", "L0_xattn_Wk", "L0_xattn_Wv", "L0_xattn_Wo", "L0_xattn_bo",
        "L0_xattn_gamma", "L0_xattn_beta"]
_OUTS = [((8, 256, 256), "float32")]


def kernel(**inputs):
    import numpy as _np
    import concourse.bacc as _bacc
    from concourse import mybir as _mybir
    from concourse.bass_utils import run_bass_kernel_spmd as _run

    nc = _bacc.Bacc("TRN2", target_bir_lowering=False, num_devices=1)
    arrays, args = {}, []
    for name in _INS:
        a = _np.ascontiguousarray(inputs[name])
        arrays[f"in_{name}_dram"] = a
        args.append(nc.dram_tensor(f"in_{name}_dram", a.shape, _mybir.dt.from_np(a.dtype), kind="ExternalInput").ap())
    for i, (shape, dtype) in enumerate(_OUTS):
        dt = _mybir.dt.from_np(_np.dtype(dtype))
        args.append(nc.dram_tensor(f"out_{i}_dram", shape, dt, kind="ExternalOutput").ap())
    cross_attention_block(nc, *args)
    r = _run(nc, [arrays], core_ids=[0])
    return r.results[0]["out_0_dram"]
```

```python
import concourse.bass as bass
from concourse import mybir
from contextlib import ExitStack


def cross_attention_block(nc, x, ctx_in, w_q, w_k, w_v, w_o, b_o, gamma, beta, out):
    fp32 = mybir.dt.float32
    fp32r = mybir.dt.float32r
    ALU = mybir.AluOpType
    ACT = mybir.ActivationFunctionType
    AX = mybir.AxisListType.X

    P = 128
    SEQS, ROWS, D = x.shape
    D_CTX = ctx_in.shape[2]
    INNER = w_q.shape[1]
    HEAD = 64
    HALF = P // 2
    PAIRS = INNER // P
    STEPS = SEQS * PAIRS
    RT = ROWS // P
    DT = D // P
    EPS = 1e-5
    SCALE = HEAD ** -0.5
    GROUP = 4
    RING = 4
    PROJECT, TURN, MIX, OUT = 2, 1, 2, 3
    LOOP_FROM, LOOP_STEPS, LOOPS = 4, 2 * PAIRS, 3
    FIRST, LAST = -10, STEPS + OUT + 1

    CT = 2 * D_CTX // P
    CREST = D_CTX - P

    x_v = x.rearrange("b (r p) d -> b p r d", p=P)
    c_v = ctx_in.rearrange("b (r p) d -> b p r d", p=P)
    y_v = out.rearrange("b (r p) d -> b p r d", p=P)

    K0, Q0, V0, O0, TILES = 0, 3, 5, 8, 10
    LO_OF = {0: 0, 1: 1, 3: 2, 4: 3, 5: 4, 6: 5, 8: 6, 9: 7}
    PIECE = INNER // 2
    PIECES = [(i, half) for half in range(2) for i in range(O0)]
    PIECES += [(i, half) for i in range(O0, TILES) for half in range(2)]
    WARM = 6
    RAWS = 10
    HI_SCALAR = {-10: (0, 1, 2), -7: (3, 4), -5: (5, 6, 7), -1: (8, 9, 10), 0: (11, 12), 1: (13,),
                 2: (14, 15, 16, 17), 3: (18, 19)}
    LO_VECTOR = {-9: (0, 1), -7: (4,), -5: (5, 6)}
    LO_POOL = {-7: (3,), -1: (8, 9, 11, 12), 0: (13, 14), 1: (16, 17), 3: (18, 19)}
    LOAD_LATE = {-3: (10, 11), -2: (12, 13), -1: (14, 15), 0: (16, 17), 1: (18, 19)}

    with ExitStack() as ctx:
        def sb(name, shape, dt=fp32):
            return ctx.enter_context(nc.sbuf_tensor(name, shape, dt))

        def bank(name):
            return ctx.enter_context(nc.psum_tensor(name, [P, 512], fp32))

        def sem(name):
            return ctx.enter_context(nc.semaphore(name))

        w_raw = sb("w_raw", [P, RAWS, PIECE])
        w_hi = sb("w_hi", [P, TILES, INNER], fp32r)
        w_lo = sb("w_lo", [P, len(LO_OF), INNER], fp32r)
        ident = sb("ident", [P, P])
        gamma_c = sb("gamma_c", [P, DT])
        beta_c = sb("beta_c", [P, DT])
        bo_b = sb("bo_b", [P, D])
        neg_half = sb("neg_half", [P, RT])
        x_in = sb("x_in", [P, 2, RT, D])
        c_in = sb("c_in", [P, 2, RT, D_CTX])
        bn = sb("bn", [P, RT, 6])
        mean_var = sb("mean_var", [P, RT, 2])
        var_eps = sb("var_eps", [P, RT])
        rstd = sb("rstd", [P, RT])
        x_norm = sb("x_norm", [P, RT, D])
        x_bias = sb("x_bias", [P, 2, RT, D])
        c_split = sb("c_split", [P, RT, 2 * D_CTX], fp32r)
        h_full = sb("h_full", [P, DT, ROWS])
        h_hi = sb("h_hi", [P, 2, DT, ROWS], fp32r)
        h_lo = sb("h_lo", [P, 2, DT, ROWS], fp32r)
        c_t = sb("c_t", [P, 2, CT, ROWS], fp32r)
        stack = sb("stack", [P, RING * 2, 3, ROWS], fp32r)
        v_sb = sb("v_sb", [P, 2, RT, GROUP * P])
        neg_max = sb("neg_max", [P, RING * 2, RT])
        sums = sb("sums", [P, RING * 2, RT])
        inv = sb("inv", [P, RING * 2, RT])
        prob = sb("prob", [P, RING * 2, RT, ROWS])
        prob_t = sb("prob_t", [P, 2, 2, RT, ROWS])
        mix_hi = sb("mix_hi", [P, 2, ROWS], fp32r)
        mix_lo = sb("mix_lo", [P, 2, ROWS], fp32r)
        y_sb = sb("y_sb", [P, 2, RT, D])

        qk_ps = bank("qk_ps")
        misc_ps = bank("misc_ps")
        s_ps = [bank("s_even_ps"), bank("s_odd_ps")]
        pt_ps = [bank("pt_even_ps"), bank("pt_odd_ps")]
        mix_ps = bank("mix_ps")
        o_ps = bank("o_ps")

        w_in = [sem(f"w_in{i}") for i in range(len(PIECES))]
        x_loaded = [sem("x_loaded0"), sem("x_loaded1")]
        c_loaded = [sem("c_loaded0"), sem("c_loaded1")]
        small_in = sem("small_in")
        ident_zero = sem("ident_zero")
        consts_ready = sem("consts_ready")
        w_hi_ready = sem("w_hi_ready")
        w_lo_ready = sem("w_lo_ready")
        w_lo_pool_ready = sem("w_lo_pool_ready")
        stats_done = sem("stats_done")
        aggr_done = sem("aggr_done")
        var_ready = sem("var_ready")
        rstd_ready = sem("rstd_ready")
        x_norm_ready = sem("x_norm_ready")
        x_bias_ready = sem("x_bias_ready")
        c_hi_ready = sem("c_hi_ready")
        c_split_ready = sem("c_split_ready")
        x_turned = sem("x_turned")
        c_turned = sem("c_turned")
        h_full_ready = sem("h_full_ready")
        h_hi_ready = sem("h_hi_ready")
        h_lo_ready = sem("h_lo_ready")
        c_t_ready = sem("c_t_ready")
        projected = sem("projected")
        hi_ready = sem("hi_ready")
        lo_ready = sem("lo_ready")
        twice = [sem(f"twice{i}") for i in range(RING)]
        v_made = sem("v_made")
        v_ready = [sem("v_ready0"), sem("v_ready1")]
        scores_made = sem("scores_made")
        max_ready = sem("max_ready")
        prob_ready = sem("prob_ready")
        inv_ready = sem("inv_ready")
        scaled = sem("scaled")
        turned = sem("turned")
        prob_t_ready = [sem("prob_t_ready_even"), sem("prob_t_ready_odd")]
        mixed = sem("mixed")
        mix_hi_ready = sem("mix_hi_ready")
        mix_lo_ready = sem("mix_lo_ready")
        o_added = sem("o_added")
        y_ready = sem("y_ready")
        y_free = [sem("y_free0"), sem("y_free1")]

        block = ctx.enter_context(nc.Block())

        def when(s, offset, every, count):
            n, rest = divmod(s - offset, every)
            return n if rest == 0 and 0 <= n < count else None

        def walk(engine, step):
            for s in range(FIRST, LOOP_FROM):
                step(s, lambda n: 0)
            with engine.Fori(0, LOOPS) as turn:
                for s in range(LOOP_FROM, LOOP_FROM + LOOP_STEPS):
                    step(s, lambda n: turn * n)
            for s in range(LOOP_FROM + LOOP_STEPS * LOOPS, LAST):
                step(s, lambda n: 0)

        def through(tile, half):
            return PIECES.index((tile, half)) + 1

        def before(n, pieces):
            return sum(1 for step in pieces.values() for piece in step if piece < n)

        def weights_ready(engine, n):
            engine.wait_ge(w_hi_ready, n)
            if before(n, LO_VECTOR):
                engine.wait_ge(w_lo_ready, before(n, LO_VECTOR))
            if before(n, LO_POOL):
                engine.wait_ge(w_lo_pool_ready, before(n, LO_POOL))

        LOAD, STATS, SPLIT_C, TURN_X, TURN_C, BIAS_X, TURN_C2 = -12, -10, -9, -8, -7, -5, -4
        PUT = PAIRS - 1 + OUT

        @block.sync
        def _(sp):
            def load_weight(n):
                if n >= RAWS:
                    weights_ready(sp, n - RAWS + 1)
                i, half = PIECES[n]
                dst = w_raw[:, n % RAWS, :]
                cols = slice(half * PIECE, (half + 1) * PIECE)
                if i in (Q0, Q0 + 1):
                    sp.dma_start(dst, w_q[(i - Q0) * P:(i - Q0 + 1) * P, cols])\
                        .then_inc(w_in[n], 16)
                elif i < O0:
                    w, k = (w_k, i - K0) if i < Q0 else (w_v, i - V0)
                    if k == 0:
                        sp.dma_start(dst, w[0:P, cols]).then_inc(w_in[n], 16)
                    elif k == 1:
                        sp.dma_start(dst[0:CREST, :], w[P:D_CTX, cols]).then_inc(w_in[n], 16)
                        sp.dma_start(dst[CREST:P, :], w[0:P - CREST, cols]).then_inc(w_in[n], 16)
                    else:
                        sp.dma_start(dst, w[D_CTX - P:D_CTX, cols]).then_inc(w_in[n], 16)
                else:
                    first = ((i - O0) * GROUP + half * GROUP // 2) * P
                    rows = w_o[first:first + GROUP // 2 * P, :]
                    sp.dma_start(dst.rearrange("p (g n) -> p g n", g=GROUP // 2),
                                 rows.rearrange("(g p) n -> p g n", p=P)).then_inc(w_in[n], 16)

            def load_x(b, sequence):
                k = b % 2
                sp.dma_start(x_in[:, k, :, :], x_v[sequence]).then_inc(x_loaded[k], 16)

            def load_c(b, sequence):
                k = b % 2
                sp.dma_start(c_in[:, k, :, :], c_v[sequence]).then_inc(c_loaded[k], 16)

            def number(n):
                return n if isinstance(n, int) else sp.snap(n)

            load_x(0, 0)
            load_c(0, 0)
            for n in range(O0):
                load_weight(n)
            load_x(1, 1)
            load_c(1, 1)
            for n in range(O0, RAWS):
                load_weight(n)

            def step(s, turns):
                for n in LOAD_LATE.get(s, ()) if s < -2 else ():
                    load_weight(n)
                b = when(s, LOAD, PAIRS, SEQS)
                if b is not None and b >= 2:
                    sequence, used = number(b + turns(2)), number(b - 1 + turns(2))
                    sp.wait_ge(x_norm_ready, used)
                    sp.wait_ge(x_bias_ready, used)
                    sp.wait_ge(c_split_ready, used)
                    load_x(b, sequence)
                    load_c(b, sequence)
                t = when(s, -PROJECT, 1, STEPS)
                if t is not None:
                    for h in range(2):
                        k = t % RING * 2 + h
                        own = slice(h * HALF, (h + 1) * HALF)
                        other = slice((1 - h) * HALF, (2 - h) * HALF)
                        split = number(4 * t + 1 + h + turns(64))
                        sp.wait_ge(lo_ready, split)
                        sp.dma_start(stack[other, k, 1:3, :].bitcast(fp32),
                                     stack[own, k, 1:3, :].bitcast(fp32))\
                            .then_inc(twice[t % RING], 16)
                for n in LOAD_LATE.get(s, ()) if s >= -2 else ():
                    load_weight(n)
                b = when(s, PUT + 1, PAIRS, SEQS)
                if b is not None:
                    sequence, added = number(b + turns(2)), number(b + 1 + turns(2))
                    sp.wait_ge(y_ready, added)
                    sp.dma_start(y_v[sequence], y_sb[:, b % 2, :, :])\
                        .then_inc(y_free[b % 2], 16)

            walk(sp, step)
            for k in range(2):
                sp.wait_ge(y_free[k], 16 * (SEQS // 2 + 1))

        @block.gpsimd
        def _(pool):
            pool.dma_start(gamma_c[:, :], gamma.rearrange("(t p) -> p t", p=P),
                           allow_slow_non_contiguous=True).then_inc(small_in, 16)
            pool.dma_start(beta_c[:, :], beta.rearrange("(t p) -> p t", p=P),
                           allow_slow_non_contiguous=True).then_inc(small_in, 16)
            pool.dma_start(bo_b[:, :], b_o.partition_broadcast(P)).then_inc(small_in, 16)
            nc.gpsimd.memset(ident[:, :], 0.0).then_inc(ident_zero, 1)
            nc.gpsimd.memset(neg_half[:, :], -0.5).then_inc(ident_zero, 1)
            pool.wait_ge(ident_zero, 2)
            nc.gpsimd.affine_select(out=ident[:, :], in_=ident[:, :], compare_op=ALU.not_equal,
                                    fill=1.0, base=0, pattern=[[-1, P]], channel_multiplier=1)\
                .then_inc(consts_ready, 1)

            def step(s, turns):
                b = when(s, STATS, PAIRS, SEQS)
                if b is not None:
                    pool.wait_ge(var_ready, b + 1 + turns(2))
                    nc.gpsimd.tensor_tensor(rstd[:, :], var_eps[:, :], neg_half[:, :], ALU.pow)\
                        .then_inc(rstd_ready, 1)
                t = when(s, 0, 1, STEPS)
                if t is not None:
                    for h in range(2):
                        k = t % RING * 2 + h
                        pool.wait_ge(inv_ready, 2 * t + h + 1 + turns(32))
                        for r in range(RT):
                            last = nc.gpsimd.tensor_scalar(prob[:, k, r, :], prob[:, k, r, :],
                                                           inv[:, k, r:r + 1], SCALE,
                                                           ALU.mult, ALU.mult)
                        last.then_inc(scaled, 1)
                for n in LO_POOL.get(s, ()):
                    i, half = PIECES[n]
                    cols = slice(half * PIECE, (half + 1) * PIECE)
                    pool.wait_ge(w_hi_ready, n + 1)
                    nc.gpsimd.tensor_tensor(w_lo[:, LO_OF[i], cols], w_raw[:, n % RAWS, :],
                                            w_hi[:, i, cols].bitcast(fp32), ALU.subtract)\
                        .then_inc(w_lo_pool_ready, 1)
                b = when(s, SPLIT_C, PAIRS, SEQS)
                if b is not None and b > 0:
                    pool.wait_ge(c_hi_ready, b + 1 + turns(2))
                    for r in range(RT):
                        last = nc.gpsimd.tensor_tensor(c_split[:, r, D_CTX:2 * D_CTX],
                                                       c_in[:, b % 2, r, :],
                                                       c_split[:, r, 0:D_CTX].bitcast(fp32),
                                                       ALU.subtract)
                    last.then_inc(c_split_ready, 1)
                b = when(s, TURN_X + 1, PAIRS, SEQS)
                if b is not None and b > 0:
                    pool.wait_ge(h_hi_ready, b + 1 + turns(2))
                    for d in range(DT):
                        last = nc.gpsimd.tensor_tensor(h_lo[:, b % 2, d, :], h_full[:, d, :],
                                                       h_hi[:, b % 2, d, :].bitcast(fp32),
                                                       ALU.subtract)
                    last.then_inc(h_lo_ready, 1)
                b = when(s, BIAS_X, PAIRS, SEQS)
                if b is not None:
                    if b == 0:
                        pool.wait_ge(small_in, 48)
                    if b >= 2:
                        pool.wait_ge(y_ready, b - 1 + turns(2))
                    for r in range(RT):
                        last = nc.gpsimd.tensor_tensor(x_bias[:, b % 2, r, :],
                                                       x_in[:, b % 2, r, :], bo_b[:, :],
                                                       ALU.add)
                    last.then_inc(x_bias_ready, 1)

            for s in range(FIRST, LAST):
                step(s, lambda n: 0)

        @block.scalar
        def _(act):
            def weight_hi(n):
                i, half = PIECES[n]
                act.wait_ge(w_in[n], 32 if i in (K0 + 1, V0 + 1) else 16)
                nc.scalar.activation(w_hi[:, i, half * PIECE:(half + 1) * PIECE],
                                     w_raw[:, n % RAWS, :], ACT.Copy).then_inc(w_hi_ready, 1)

            def step(s, turns):
                t = when(s, OUT, 1, STEPS)
                if t is not None:
                    act.wait_ge(mixed, t + 1 + turns(16))
                    nc.scalar.activation(mix_hi[:, t % 2, :], mix_ps[:, 0:ROWS], ACT.Copy)\
                        .then_inc(mix_hi_ready, 1)

                b = when(s, TURN_X + 1, PAIRS, SEQS)
                if b is not None:
                    if b == 0:
                        act.wait_ge(small_in, 48)
                    if b >= 1:
                        act.wait_ge(h_lo_ready, b + turns(2))
                    act.wait_ge(x_turned, b + 1 + turns(2))
                    for d in range(DT):
                        last = nc.scalar.activation(h_full[:, d, :],
                                                    misc_ps[:, d * ROWS:(d + 1) * ROWS],
                                                    ACT.Identity, bias=beta_c[:, d:d + 1],
                                                    scale=gamma_c[:, d:d + 1])
                    last.then_inc(h_full_ready, 1)
                g = when(s, -1, GROUP, STEPS // GROUP)
                if g is not None:
                    act.wait_ge(v_made, 2 * g + 1 + turns(8))
                    nc.scalar.activation(v_sb[:, g % 2, 0, :], misc_ps[:, :], ACT.Copy)\
                        .then_inc(v_ready[0], 1)

                if s == TURN_C:
                    act.wait_ge(c_turned, 1)
                    nc.scalar.activation(c_t[:, 0, 0:2, :].rearrange("p a b -> p (a b)"),
                                         pt_ps[0][:, :], ACT.Copy).then_inc(c_t_ready, 1)

                for n in HI_SCALAR.get(s, ()):
                    weight_hi(n)

                t = when(s, MIX, 1, STEPS)
                if t is not None:
                    if t >= 2:
                        act.wait_ge(mixed, t - 1 + turns(16))
                    act.wait_ge(turned, 2 * t + 1 + turns(32))
                    nc.scalar.activation(prob_t[:, t % 2, 0, :, :].rearrange("p a b -> p (a b)"),
                                         pt_ps[0][:, :], ACT.Copy).then_inc(prob_t_ready[0], 1)

                def probabilities(h):
                    t = when(s, 0, 1, STEPS)
                    if t is not None:
                        k = t % RING * 2 + h
                        if t >= RING:
                            act.wait_ge(turned, 2 * (t - RING) + h + 1 + turns(32))
                        act.wait_ge(max_ready, 2 * t + h + 1 + turns(32))
                        for r in range(RT):
                            last = nc.scalar.activation(prob[:, k, r, :],
                                                        s_ps[h][:, r * ROWS:(r + 1) * ROWS],
                                                        ACT.Exp, bias=neg_max[:, k, r:r + 1],
                                                        accum_out=sums[:, k, r:r + 1])
                        last.then_inc(prob_ready, 1)

                probabilities(0)

                t = when(s, -PROJECT, 1, STEPS)
                if t is not None:
                    if t >= RING:
                        act.wait_ge(scores_made, 2 * (t - RING) + 2 + turns(32))
                    act.wait_ge(projected, t + 1 + turns(16))
                    for h in range(2):
                        rows = slice(h * HALF, (h + 1) * HALF)
                        nc.scalar.activation(stack[rows, t % RING * 2 + h, 0:2, :]
                                             .rearrange("p a b -> p (a b)"),
                                             qk_ps[rows, :], ACT.Copy).then_inc(hi_ready, 1)

                if s == -1:
                    act.wait_ge(v_made, 2)
                    nc.scalar.activation(v_sb[:, 0, 1, :], misc_ps[:, :], ACT.Copy)\
                        .then_inc(v_ready[1], 1)

                probabilities(1)

            walk(act, step)

        @block.vector
        def _(dve):
            for k in range(2):
                nc.vector.memset(y_sb[:, k, :, :], 0.0).then_inc(y_free[k], 16)

            def weight_lo(n):
                i, half = PIECES[n]
                cols = slice(half * PIECE, (half + 1) * PIECE)
                dve.wait_ge(w_hi_ready, n + 1)
                nc.vector.tensor_tensor(w_lo[:, LO_OF[i], cols], w_raw[:, n % RAWS, :],
                                        w_hi[:, i, cols].bitcast(fp32), ALU.subtract)\
                    .then_inc(w_lo_ready, 1)

            def step(s, turns):
                b = when(s, PUT + 1, PAIRS, SEQS)
                if b is not None:
                    k = b % 2
                    dve.wait_ge(y_free[k], 16 * (b // 2 + 1) + turns(16))
                    dve.wait_ge(x_bias_ready, b + 1 + turns(2))
                    dve.wait_ge(o_added, PAIRS * (b + 1) + turns(16))
                    nc.vector.tensor_tensor(y_sb[:, k, :, :].rearrange("p a b -> p (a b)"), o_ps[:, :],
                                            x_bias[:, k, :, :].rearrange("p a b -> p (a b)"),
                                            ALU.add).then_inc(y_ready, 1)

                t = when(s, OUT, 1, STEPS)
                if t is not None:
                    dve.wait_ge(mix_hi_ready, t + 1 + turns(16))
                    nc.vector.tensor_tensor(mix_lo[:, t % 2, :], mix_ps[:, 0:ROWS],
                                            mix_hi[:, t % 2, :].bitcast(fp32), ALU.subtract)\
                        .then_inc(mix_lo_ready, 1)

                t = when(s, 1, 1, STEPS)
                if t is not None:
                    for h in range(2):
                        k = t % RING * 2 + h
                        dve.wait_ge(prob_ready, 2 * t + h + 1 + turns(32))
                        nc.vector.reciprocal(inv[:, k, :], sums[:, k, :]).then_inc(inv_ready, 1)

                for part, (offset, tiles) in enumerate(((TURN_C, 2), (TURN_C2, CT - 2))):
                    b = when(s, offset + 1, PAIRS, SEQS)
                    if s == TURN_C and part == 1:
                        dve.wait_ge(c_turned, 2)
                        nc.vector.tensor_copy(c_t[:, 0, 2:CT, :].rearrange("p a b -> p (a b)"),
                                              pt_ps[1][:, 0:(CT - 2) * ROWS]).then_inc(c_t_ready, 1)
                    if b is not None and b > 0:
                        dve.wait_ge(c_turned, 2 * b + part + 1 + turns(4))
                        nc.vector.tensor_copy(c_t[:, b % 2, 2 * part:2 * part + tiles, :]
                                              .rearrange("p a b -> p (a b)"),
                                              misc_ps[:, 0:tiles * ROWS]).then_inc(c_t_ready, 1)
                g = when(s, 0, GROUP, STEPS // GROUP)
                if g is not None and g > 0:
                    dve.wait_ge(v_made, 2 * g + 2 + turns(8))
                    nc.vector.tensor_copy(v_sb[:, g % 2, 1, :], misc_ps[:, :])\
                        .then_inc(v_ready[1], 1)

                t = when(s, 0, 1, STEPS)
                if t is not None:
                    for h in range(2):
                        dve.wait_ge(scores_made, 2 * t + h + 1 + turns(32))
                        nc.vector.tensor_reduce(neg_max[:, t % RING * 2 + h, :],
                                                s_ps[h][:, :].rearrange("p (r j) -> p r j", r=RT),
                                                AX, ALU.max, negate=True).then_inc(max_ready, 1)

                t = when(s, MIX, 1, STEPS)
                if t is not None:
                    if t >= 2:
                        dve.wait_ge(mixed, t - 1 + turns(16))
                    dve.wait_ge(turned, 2 * t + 2 + turns(32))
                    nc.vector.tensor_copy(prob_t[:, t % 2, 1, :, :].rearrange("p a b -> p (a b)"),
                                          pt_ps[1][:, :]).then_inc(prob_t_ready[1], 1)

                def prepare():
                    b = when(s, STATS, PAIRS, SEQS)
                    if b is not None:
                        k = b % 2
                        dve.wait_ge(x_loaded[k], 16 * (b // 2 + 1) + turns(16))
                        for r in range(RT):
                            last = nc.vector.bn_stats(bn[:, r, :], x_in[:, k, r, :])
                        last.then_inc(stats_done, 1)
                        dve.wait_ge(stats_done, b + 1 + turns(2))
                        nc.vector.memset(var_eps[:, :], 0.0)
                        for r in range(RT):
                            last = nc.vector.bn_aggr(mean_var[:, r, :], bn[:, r, :])
                        last.then_inc(aggr_done, 1)
                        dve.wait_ge(aggr_done, b + 1 + turns(2))
                        nc.vector.tensor_scalar(var_eps[:, :], mean_var[:, :, 1], EPS, None, ALU.add)\
                            .then_inc(var_ready, 1)

                    b = when(s, STATS + 1, PAIRS, SEQS)
                    if b is not None:
                        if b >= 1:
                            dve.wait_ge(x_turned, b + turns(2))
                        dve.wait_ge(rstd_ready, b + 1 + turns(2))
                        for r in range(RT):
                            last = nc.vector.tensor_scalar(x_norm[:, r, :], x_in[:, b % 2, r, :],
                                                           mean_var[:, r, 0:1], rstd[:, r:r + 1],
                                                           ALU.subtract, ALU.mult)
                        last.then_inc(x_norm_ready, 1)

                    b = 0 if s == FIRST else when(s, SPLIT_C, PAIRS, SEQS)
                    if b is not None and (b > 0 or s == FIRST):
                        dve.wait_ge(c_loaded[b % 2], 16 * (b // 2 + 1) + turns(16))
                        if b >= 1:
                            dve.wait_ge(c_turned, 2 * b + turns(4))
                        nc.vector.tensor_copy(c_split[:, :, 0:D_CTX], c_in[:, b % 2, :, :])\
                            .then_inc(c_hi_ready, 1)
                        if b == 0:
                            dve.wait_ge(c_hi_ready, 1)
                            nc.vector.tensor_tensor(c_split[:, :, D_CTX:2 * D_CTX], c_in[:, 0, :, :],
                                                    c_split[:, :, 0:D_CTX].bitcast(fp32),
                                                    ALU.subtract).then_inc(c_split_ready, 1)

                if s < 0:
                    prepare()

                def q_lo(h):
                    t = when(s, -PROJECT, 1, STEPS)
                    if t is not None:
                        k = t % RING * 2 + h
                        rows = slice(h * HALF, (h + 1) * HALF)
                        dve.wait_ge(hi_ready, 2 * t + h + 1 + turns(32))
                        nc.vector.tensor_tensor(stack[rows, k, 2, :], qk_ps[rows, ROWS:2 * ROWS],
                                                stack[rows, k, 1, :].bitcast(fp32),
                                                ALU.subtract).then_inc(lo_ready, 1)

                q_lo(0)
                q_lo(1)
                t = when(s, -PROJECT, 1, STEPS)
                if t is not None:
                    for h in range(2):
                        k = t % RING * 2 + h
                        rows = slice(h * HALF, (h + 1) * HALF)
                        other = slice((1 - h) * HALF, (2 - h) * HALF)
                        nc.vector.tensor_tensor(stack[other, k, 0, :], qk_ps[rows, 0:ROWS],
                                                stack[rows, k, 0, :].bitcast(fp32),
                                                ALU.subtract).then_inc(lo_ready, 1)

                b = when(s, TURN_X + 1, PAIRS, SEQS)
                if b is not None:
                    dve.wait_ge(h_full_ready, b + 1 + turns(2))
                    nc.vector.tensor_copy(h_hi[:, b % 2, :, :], h_full[:, :, :])\
                        .then_inc(h_hi_ready, 1)
                    if b == 0:
                        dve.wait_ge(h_hi_ready, 1)
                        nc.vector.tensor_tensor(h_lo[:, 0, :, :], h_full[:, :, :],
                                                h_hi[:, 0, :, :].bitcast(fp32),
                                                ALU.subtract).then_inc(h_lo_ready, 1)

                if s >= 0:
                    prepare()

                for n in LO_VECTOR.get(s, ()):
                    weight_lo(n)

            walk(dve, step)

        @block.tensor
        def _(pe):
            def context_products():
                return [(w_hi, k, k) for k in range(CT)] + [(w_lo, k, k) for k in range(2)]

            def keep_warm():
                for _ in range(WARM):
                    nc.tensor.transpose(o_ps[:, 0:P], ident[:, :], ident[:, :])

            def step(s, turns):
                if s == -PROJECT - 1:
                    keep_warm()

                t = when(s, 0, 1, STEPS)
                if t is not None:
                    pe.wait_ge(twice[t % RING], 32 * (t // RING + 1) + turns(128))
                    for h in range(2):
                        k = t % RING * 2 + h
                        pe.wait_ge(lo_ready, 4 * t + 3 + h + turns(64))
                        if t >= 1:
                            pe.wait_ge(prob_ready, 2 * (t - 1) + h + 1 + turns(32))
                        for r in range(RT):
                            for part in range(2):
                                last = nc.tensor.matmul(
                                    s_ps[h][:, r * ROWS:(r + 1) * ROWS],
                                    stack[:, k, 1 + part, r * P:(r + 1) * P], stack[:, k, 0, :],
                                    start=part == 0, stop=part == 1)
                        last.then_inc(scores_made, 1)

                t = when(s, -PROJECT, 1, STEPS)
                if t is not None:
                    b, p = divmod(t, PAIRS)
                    k = b % 2
                    cols = slice(p * P, (p + 1) * P)
                    if t in (0, GROUP):
                        weights_ready(pe, through(Q0 - 1, t // GROUP))
                    if p == 0:
                        pe.wait_ge(c_t_ready, 2 * b + 2 + turns(4))
                    if t >= 1:
                        pe.wait_ge(lo_ready, 4 * t + turns(64))
                    passes = context_products()
                    for n, (w, wk, ck) in enumerate(passes):
                        nc.tensor.matmul(qk_ps[:, 0:ROWS], w[:, K0 + wk, cols], c_t[:, k, ck, :],
                                         start=n == 0, stop=n == len(passes) - 1)
                    if p == 0:
                        pe.wait_ge(h_lo_ready, b + 1 + turns(2))
                    if t in (0, GROUP):
                        weights_ready(pe, through(V0 - 1, t // GROUP))
                    passes = [(w, d, h) for w, h in ((w_hi, h_hi), (w_hi, h_lo), (w_lo, h_hi))
                              for d in range(DT)]
                    for n, (w, d, h) in enumerate(passes):
                        wk = Q0 + d if w is w_hi else LO_OF[Q0 + d]
                        last = nc.tensor.matmul(qk_ps[:, ROWS:2 * ROWS], w[:, wk, cols],
                                                h[:, k, d, :], start=n == 0, stop=n == len(passes) - 1)
                    last.then_inc(projected, 1)

                t = when(s, OUT, 1, STEPS)
                if t is not None:
                    b, p = divmod(t, PAIRS)
                    if t in (0, GROUP):
                        weights_ready(pe, through(O0 + t // GROUP, 1))
                    if p == 0 and b >= 1:
                        pe.wait_ge(y_ready, b + turns(2))
                    pe.wait_ge(mix_lo_ready, t + 1 + turns(16))
                    o, cols = divmod(p, GROUP)
                    cols = slice(cols * D, (cols + 1) * D)
                    for r in range(RT):
                        passes = [(mix_hi, w_hi, O0 + o), (mix_lo, w_hi, O0 + o),
                                  (mix_hi, w_lo, LO_OF[O0 + o])]
                        for n, (m, w, wk) in enumerate(passes):
                            last = nc.tensor.matmul(o_ps[:, r * D:(r + 1) * D],
                                                    m[:, t % 2, r * P:(r + 1) * P],
                                                    w[:, wk, cols],
                                                    start=p == 0 and n == 0 and r == 0,
                                                    stop=p == PAIRS - 1 and n == 2,
                                                    skip_group_check=True)
                    last.then_inc(o_added, 1)

                b = when(s, TURN_X, PAIRS, SEQS)
                if b is not None:
                    if b >= 1:
                        pe.wait_ge(v_ready[1], 2 * (b - 1) + 1 + turns(4))
                    pe.wait_ge(x_norm_ready, b + 1 + turns(2))
                    for d in range(DT):
                        for r in range(RT):
                            last = nc.tensor.transpose(
                                misc_ps[:, d * ROWS + r * P:d * ROWS + (r + 1) * P],
                                x_norm[:, r, d * P:(d + 1) * P], ident[:, :])
                    last.then_inc(x_turned, 1)

                for part, (offset, tiles) in enumerate(((TURN_C, 2), (TURN_C2, CT - 2))):
                    b = 0 if s == TURN_C else when(s, offset, PAIRS, SEQS)
                    if b is not None and (b > 0 or s == TURN_C):
                        bank_ps = misc_ps if b > 0 else pt_ps[part]
                        if b > 0 and part == 0:
                            pe.wait_ge(h_full_ready, b + 1 + turns(2))
                        elif b > 0:
                            pe.wait_ge(v_ready[1], 2 * b + turns(4))
                        pe.wait_ge(c_split_ready, b + 1 + turns(2))
                        for n in range(tiles):
                            cols = slice((2 * part + n) * P, (2 * part + n + 1) * P)
                            for r in range(RT):
                                last = nc.tensor.transpose(
                                    bank_ps[:, n * ROWS + r * P:n * ROWS + (r + 1) * P],
                                    c_split[:, r, cols].bitcast(fp32), ident[:, :])
                        last.then_inc(c_turned, 1)

                for j in range(RT):
                    g = when(s, j - 2, GROUP, STEPS // GROUP)
                    if g is not None:
                        b, half = divmod(g, 2)
                        if s in (-2, GROUP - 2):
                            weights_ready(pe, through(O0 - 1, g))
                        if j == 1:
                            pe.wait_ge(v_ready[0], g + 1 + turns(4))
                        elif half == 0:
                            pe.wait_ge(c_t_ready, 2 * b + 2 + turns(4))
                        elif b + 1 < SEQS:
                            pe.wait_ge(c_t_ready, 2 * b + 3 + turns(4))
                        else:
                            pe.wait_ge(v_ready[1], g)
                        cols = slice(half * GROUP * P, (half + 1) * GROUP * P)
                        passes = context_products()
                        for n, (w, wk, ck) in enumerate(passes):
                            wk = wk + V0 if w is w_hi else LO_OF[V0 + wk]
                            last = nc.tensor.matmul(misc_ps[:, :],
                                                    c_t[:, b % 2, ck, j * P:(j + 1) * P],
                                                    w[:, wk, cols],
                                                    start=n == 0, stop=n == len(passes) - 1)
                        last.then_inc(v_made, 1)

                t = when(s, MIX, 1, STEPS)
                if t is not None:
                    g, p = divmod(t, GROUP)
                    if p == 0:
                        for j in range(RT):
                            pe.wait_ge(v_ready[j], g + 1 + turns(4))
                    if t >= 1:
                        pe.wait_ge(mix_lo_ready, t + turns(16))
                    for j in range(RT):
                        for h in range(2):
                            if j == 0:
                                pe.wait_ge(prob_t_ready[h], t + 1 + turns(16))
                            last = nc.tensor.matmul(
                                mix_ps[h * HALF:(h + 1) * HALF, 0:ROWS],
                                v_sb[:, g % 2, j, p * P + h * HALF:p * P + (h + 1) * HALF],
                                prob_t[:, t % 2, h, j, :], start=j == 0, stop=j == RT - 1)
                    last.then_inc(mixed, 1)

                t = when(s, TURN, 1, STEPS)
                if t is not None:
                    for h in range(2):
                        k = t % RING * 2 + h
                        pe.wait_ge(scaled, 2 * t + h + 1 + turns(32))
                        if t >= 1:
                            pe.wait_ge(prob_t_ready[h], t + turns(16))
                        for r in range(RT):
                            for j in range(RT):
                                last = nc.tensor.transpose(
                                    pt_ps[h][:, j * ROWS + r * P:j * ROWS + (r + 1) * P],
                                    prob[:, k, r, j * P:(j + 1) * P], ident[:, :])
                        last.then_inc(turned, 1)

            pe.wait_ge(consts_ready, 1)
            keep_warm()
            walk(pe, step)


_INS = ["x", "ctx_768", "L0_xattn_Wq", "L0_xattn_Wk", "L0_xattn_Wv", "L0_xattn_Wo", "L0_xattn_bo",
        "L0_xattn_gamma", "L0_xattn_beta"]
_OUTS = [((8, 256, 256), "float32")]


def kernel(**inputs):
    import numpy as _np
    import concourse.bacc as _bacc
    from concourse import mybir as _mybir
    from concourse.bass_utils import run_bass_kernel_spmd as _run

    nc = _bacc.Bacc("TRN2", target_bir_lowering=False, num_devices=1)
    arrays, args = {}, []
    for name in _INS:
        a = _np.ascontiguousarray(inputs[name])
        arrays[f"in_{name}_dram"] = a
        args.append(nc.dram_tensor(f"in_{name}_dram", a.shape, _mybir.dt.from_np(a.dtype), kind="ExternalInput").ap())
    for i, (shape, dtype) in enumerate(_OUTS):
        dt = _mybir.dt.from_np(_np.dtype(dtype))
        args.append(nc.dram_tensor(f"out_{i}_dram", shape, dt, kind="ExternalOutput").ap())
    cross_attention_block(nc, *args)
    r = _run(nc, [arrays], core_ids=[0])
    return r.results[0]["out_0_dram"]
```
